# Optimizing a Trainium2 kernel written in Bass

```python
import numpy as np
import jax
import jax.numpy as jnp

def _softmax(x, axis=-1):
    return jax.nn.softmax(x, axis=axis)

def _gelu(x):
    return jax.nn.gelu(x, approximate=True)

def _silu(x):
    return jax.nn.silu(x)

def _sigmoid(x):
    return jax.nn.sigmoid(x)

def _layernorm(x, axis=-1, eps=1e-05):
    m = jnp.mean(x, axis=axis, keepdims=True)
    v = jnp.var(x, axis=axis, keepdims=True)
    return (x - m) / jnp.sqrt(v + eps)

def _scatter_add(tgt, idx, src, axis=0):
    return tgt.at[idx].add(src)

def _segment_sum(src, seg, n):
    return jax.ops.segment_sum(src, seg, n)
kernel_name = 'mk_adaln_d1_jaxref_r8_40eb2f'

def setup_inputs(seed: int=0):
    np.random.seed(seed)
    _w = jnp.asarray

    def _L0_attn_setup():
        import jax, jax.numpy as jnp
        import numpy as np
        N_Q, N_KV = (16, 4)

        def _rope(x):
            d = x.shape[-1]
            T = x.shape[-2]
            inv_freq = 1.0 / 10000.0 ** (jnp.arange(d // 2, dtype=jnp.float32) * 2.0 / d)
            emb = jnp.arange(T, dtype=jnp.float32)[:, None] * inv_freq[None, :]
            cos, sin = (jnp.cos(emb), jnp.sin(emb))
            x1, x2 = (x[..., 0::2], x[..., 1::2])
            return jnp.concatenate([x1 * cos - x2 * sin, x1 * sin + x2 * cos], axis=-1)
        key = jax.random.key(seed)
        ks = jax.random.split(key, 5)
        B, T, C = (4, 256, 256)
        g = N_Q // N_KV
        Ckv = C // g
        s = 0.02
        return {'x': jax.random.normal(ks[0], (B, T, C), dtype=jnp.float32), 'Wq': jax.random.normal(ks[1], (C, C), dtype=jnp.float32) * s, 'bq': jnp.zeros((C,), dtype=jnp.float32), 'Wk': jax.random.normal(ks[2], (C, Ckv), dtype=jnp.float32) * s, 'bk': jnp.zeros((Ckv,), dtype=jnp.float32), 'Wv': jax.random.normal(ks[3], (C, Ckv), dtype=jnp.float32) * s, 'bv': jnp.zeros((Ckv,), dtype=jnp.float32), 'Wo': jax.random.normal(ks[4], (Ckv, C), dtype=jnp.float32) * s, 'bo': jnp.zeros((C,), dtype=jnp.float32)}
    _L0_attn_in = _L0_attn_setup()

    def _L0_ffn_setup():
        import jax, jax.numpy as jnp
        import numpy as np
        B, T, D, FF = (4, 256, 256, 704)
        EPS = 1e-06

        def rmsnorm(x, w):
            var = jnp.mean(jnp.square(x), axis=-1, keepdims=True)
            return x * jax.lax.rsqrt(var + EPS) * w
        key = jax.random.key(seed)
        ks = jax.random.split(key, 9)
        s = 0.02
        return {'hidden_states': jax.random.normal(ks[0], (B, T, D), jnp.float32), 'w_router': jax.random.normal(ks[1], (D,), jnp.float32) * s, 'b_router': jnp.zeros((), jnp.float32), 'norm1_w': jnp.ones((D,), jnp.float32), 'wv': jax.random.normal(ks[2], (D, D), jnp.float32) * s, 'bv': jnp.zeros((D,), jnp.float32), 'wo': jax.random.normal(ks[3], (D, D), jnp.float32) * s, 'norm2_w': jnp.ones((D,), jnp.float32), 'w_gate': jax.random.normal(ks[4], (D, FF), jnp.float32) * s, 'w_up': jax.random.normal(ks[5], (D, FF), jnp.float32) * s, 'w_down': jax.random.normal(ks[6], (FF, D), jnp.float32) * s}
    _L0_ffn_in = _L0_ffn_setup()
    _L0_c = _w((lambda *s: np.random.randn(*s).astype(np.float32) * 0.05)(4, 256))
    _L0_wmod = _w((lambda *s: np.random.randn(*s).astype(np.float32) * 0.05)(256, 6 * 256) * 256 ** (-0.5))
    _d = {'L0_attn_x': _L0_attn_in['x'], 'L0_attn_Wq': _L0_attn_in['Wq'], 'L0_attn_bq': _L0_attn_in['bq'], 'L0_attn_Wk': _L0_attn_in['Wk'], 'L0_attn_bk': _L0_attn_in['bk'], 'L0_attn_Wv': _L0_attn_in['Wv'], 'L0_attn_bv': _L0_attn_in['bv'], 'L0_attn_Wo': _L0_attn_in['Wo'], 'L0_attn_bo': _L0_attn_in['bo'], 'L0_ffn_w_router': _L0_ffn_in['w_router'], 'L0_ffn_b_router': _L0_ffn_in['b_router'], 'L0_ffn_norm1_w': _L0_ffn_in['norm1_w'], 'L0_ffn_wv': _L0_ffn_in['wv'], 'L0_ffn_bv': _L0_ffn_in['bv'], 'L0_ffn_wo': _L0_ffn_in['wo'], 'L0_ffn_norm2_w': _L0_ffn_in['norm2_w'], 'L0_ffn_w_gate': _L0_ffn_in['w_gate'], 'L0_ffn_w_up': _L0_ffn_in['w_up'], 'L0_ffn_w_down': _L0_ffn_in['w_down'], 'L0_c': _L0_c, 'L0_wmod': _L0_wmod}
    _x0 = _d['L0_attn_x']
    _d['L0_attn_x'] = jax.random.normal(jax.random.fold_in(jax.random.key(seed), 1), (4, 1024, 256), dtype=_x0.dtype)
    del _x0
    return _d

def reference(L0_attn_x, L0_attn_Wq, L0_attn_bq, L0_attn_Wk, L0_attn_bk, L0_attn_Wv, L0_attn_bv, L0_attn_Wo, L0_attn_bo, L0_ffn_w_router, L0_ffn_b_router, L0_ffn_norm1_w, L0_ffn_wv, L0_ffn_bv, L0_ffn_wo, L0_ffn_norm2_w, L0_ffn_w_gate, L0_ffn_w_up, L0_ffn_w_down, L0_c, L0_wmod):

    def _L0_attn_ref(x, Wq, bq, Wk, bk, Wv, bv, Wo, bo):
        import jax, jax.numpy as jnp
        import numpy as np
        N_Q, N_KV = (16, 4)

        def _rope(x):
            d = x.shape[-1]
            T = x.shape[-2]
            inv_freq = 1.0 / 10000.0 ** (jnp.arange(d // 2, dtype=jnp.float32) * 2.0 / d)
            emb = jnp.arange(T, dtype=jnp.float32)[:, None] * inv_freq[None, :]
            cos, sin = (jnp.cos(emb), jnp.sin(emb))
            x1, x2 = (x[..., 0::2], x[..., 1::2])
            return jnp.concatenate([x1 * cos - x2 * sin, x1 * sin + x2 * cos], axis=-1)
        B, T, C = x.shape
        g = N_Q // N_KV
        d = C // N_Q
        q = (x @ Wq + bq).reshape(B, T, N_Q, d).transpose(0, 2, 1, 3)
        k = (x @ Wk + bk).reshape(B, T, N_KV, d).transpose(0, 2, 1, 3)
        v = (x @ Wv + bv).reshape(B, T, N_KV, d).transpose(0, 2, 1, 3)
        q = _rope(q)
        k = _rope(k)
        qg = q.reshape(B, N_KV, g, T, d)
        scores = jnp.einsum('bhgnd,bhsd->bhns', qg, k) * (1.0 / jnp.sqrt(jnp.float32(d)))
        mask = jnp.tril(jnp.ones((T, T), dtype=bool))
        att = jax.nn.softmax(jnp.where(mask, scores, -jnp.inf), axis=-1)
        y = jnp.einsum('bhns,bhsd->bhnd', att, v)
        y = y.transpose(0, 2, 1, 3).reshape(B, T, C // g)
        return y @ Wo + bo

    def _L0_ffn_ref(hidden_states, w_router, b_router, norm1_w, wv, bv, wo, norm2_w, w_gate, w_up, w_down):
        import jax, jax.numpy as jnp
        import numpy as np
        B, T, D, FF = (4, 256, 256, 704)
        EPS = 1e-06

        def rmsnorm(x, w):
            var = jnp.mean(jnp.square(x), axis=-1, keepdims=True)
            return x * jax.lax.rsqrt(var + EPS) * w
        x = hidden_states
        scores = jnp.einsum('btd,d->bt', x, w_router) + b_router
        routed = jax.nn.sigmoid(scores) > 0.5
        h1 = rmsnorm(x, norm1_w)
        v = jnp.einsum('btd,de->bte', h1, wv) + bv
        attn = jnp.einsum('bte,ed->btd', v, wo)
        h = x + attn
        h2 = rmsnorm(h, norm2_w)
        mlp = jnp.einsum('btf,fd->btd', jax.nn.silu(h2 @ w_gate) * (h2 @ w_up), w_down)
        processed = h + mlp
        return jnp.where(routed[..., None], processed, x)
    x = L0_attn_x
    mod = (_silu(L0_c) @ L0_wmod).reshape(L0_c.shape[0], 6, 1, -1)
    sa, ca, ga, sb, cb, gb = (mod[:, 0], mod[:, 1], mod[:, 2], mod[:, 3], mod[:, 4], mod[:, 5])
    ga = (2 * (ga >= 0) - 1) * jnp.maximum(jnp.abs(ga), 0.25)
    gb = (2 * (gb >= 0) - 1) * jnp.maximum(jnp.abs(gb), 0.25)
    h = _layernorm(x, axis=-1) * (1 + ca) + sa
    x = x + ga * _L0_attn_ref(h, L0_attn_Wq, L0_attn_bq, L0_attn_Wk, L0_attn_bk, L0_attn_Wv, L0_attn_bv, L0_attn_Wo, L0_attn_bo)
    h = _layernorm(x, axis=-1) * (1 + cb) + sb
    x = x + gb * _L0_ffn_ref(h, L0_ffn_w_router, L0_ffn_b_router, L0_ffn_norm1_w, L0_ffn_wv, L0_ffn_bv, L0_ffn_wo, L0_ffn_norm2_w, L0_ffn_w_gate, L0_ffn_w_up, L0_ffn_w_down)
    return x

_drawn_inputs = setup_inputs


def setup_inputs(seed=0):
    import zlib

    import numpy as np

    out = dict(_drawn_inputs(seed))
    spreads = {'L0_attn_bq': (0.0, 0.8),
     'L0_attn_bk': (0.0, 0.8),
     'L0_attn_bv': (0.0, 0.8),
     'L0_attn_bo': (0.0, 0.331),
     'L0_ffn_norm1_w': (1.0, 0.6),
     'L0_ffn_bv': (0.0, 0.8),
     'L0_ffn_norm2_w': (1.0, 0.6)}
    factors = {'L0_attn_Wq': 8.0,
     'L0_attn_Wk': 8.0,
     'L0_attn_Wv': 8.0,
     'L0_attn_Wo': 8.0,
     'L0_ffn_w_router': 4.046,
     'L0_ffn_wv': 3.128,
     'L0_ffn_wo': 2.968,
     'L0_ffn_w_gate': 8.0,
     'L0_ffn_w_up': 8.0,
     'L0_ffn_w_down': 8.0}
    for name, (base, spread) in spreads.items():
        noise = np.random.default_rng([zlib.crc32(name.encode()), seed]).standard_normal(out[name].shape)
        drawn = base * np.exp(spread * noise) if base else spread * noise
        out[name] = jnp.asarray(drawn.astype(out[name].dtype))
    for name, factor in factors.items():
        out[name] = (out[name] * factor).astype(out[name].dtype)
    return out
```

```python
from contextlib import ExitStack

import concourse.bass as bass
import numpy as np
from concourse import mybir

F32 = mybir.dt.float32
F32R = mybir.dt.float32r
BF16 = mybir.dt.bfloat16
ALU = mybir.AluOpType
ACT = mybir.ActivationFunctionType
AX = mybir.AxisListType

P = 128
B, T, C = 4, 1024, 256
N_Q, H = 16, 4
G = N_Q // H
D = C // N_Q
HALF = D // 2
FF = 704
KB = C // P
NT = T // P
CH = 512
NC = T // CH
TPC = CH // P
QKV = 3 * H * D
FB = FF // P
FR = FF - FB * P
GUB = 2 * FB + 1
W1N = C + 2
QS = 3 * D
QP = 2 * QS
KR = QP + 2 * H
KSTEP = KR + QS
NEG = -1.0e30
LN_EPS, RMS_EPS = 1e-5, 1e-6

MAX_UNITS = []
for qt in range(NT):
    for k0 in range(0, (qt + 1) * P, CH):
        kn = min(CH, (qt + 1) * P - k0)
        hn = min(H, CH // kn)
        MAX_UNITS += [(qt, k0, kn, h0, hn) for h0 in range(0, H, hn)]
MAX_OF_CHUNK = [[u for u in MAX_UNITS if u[0] // TPC == c] for c in range(NC)]
P_UNITS = [(c, j, max(0, j - c * TPC) * P) for c in range(NC) for j in range((c + 1) * TPC)]

def steps():
    yield "weights", 0
    yield "norm1", 0
    for s in range(NT + 1):
        if s < NT:
            yield "xT", s
        if s >= 1:
            yield "qkv", s - 1
        if s > TPC:
            yield "stackT", s - TPC - 1
        if s >= 1 and s % TPC == 0:
            yield "rope", s // TPC - 1
    for t in range(NT - TPC, NT):
        yield "stackT", t
    for c in range(NC):
        for n in range(len(MAX_OF_CHUNK[c])):
            yield "max", (c, n)
        yield "maxrow", c
    n = 0
    for c in range(NC):
        for j in range((c + 1) * TPC):
            yield "prob", n
            if j > 0:
                yield "pv", n - 1
            if c > 0 and j == 1:
                yield "yT", c - 1
            if c > 0 and j == 2:
                yield "ynT", c - 1
            n += 1
        yield "pv", n - 1
        yield "ycopy", c
    yield "yT", NC - 1
    yield "ynT", NC - 1
    lags = (("wo", 0), ("norm2", 1), ("hT", 2), ("a", 3), ("h2", 4), ("h2T", 5))
    for s in range(NT + lags[-1][1]):
        for kind, lag in lags:
            if 0 <= s - lag < NT:
                yield kind, s - lag
    for c in range(NC):
        for i in range(FB + 1):
            yield "gateup", (c, i)
        for t in range(TPC):
            yield "down", c * TPC + t


STEPS = list(steps())
DVE_CHAIN = 1 + NT + 1 + NC + (NC - 1) + NC + NC
POOL_CHAIN = 1 + NT * 3 + NT * 2
V_CSL, V_MOD, V_FWVT = 2, 8, 9


def adaln_layer(nc, x, Wq, bq, Wk, bk, Wv, bv, Wo, bo, w_router, b_router, n1, f_wv, f_bv, f_wo, n2,
                w_gate, w_up, w_down, c_in, wmod, rope_cos, rope_sin, out):
    ctx = ExitStack()
    with ctx:
        ctx.enter_context(nc.allow_non_contiguous_dma(reason="short vectors laid over partitions"))

        def sb(name, shape, dt=F32):
            return ctx.enter_context(nc.sbuf_tensor(name, shape, dt))

        def sem(name):
            return ctx.enter_context(nc.semaphore(name))

        mod_dram = nc.dram_tensor("mod_scratch", [B, 6 * C], F32, kind="Internal").ap()

        ident = sb("ident", [P, P])
        ident_b = sb("ident_b", [P, P], BF16)
        mask_qk = sb("mask_qk", [P, P], BF16)
        mask_kq = sb("mask_kq", [P, P], BF16)
        cos_t = sb("cos_t", [P, NT, HALF])
        sin_t = sb("sin_t", [P, NT, HALF])
        expo = sb("expo", [P, NT])
        eps_ln = sb("eps_ln", [P, NT])
        eps_rms = sb("eps_rms", [P, NT])
        Wqkv = sb("Wqkv", [P, KB, QKV])
        bqkv = sb("bqkv", [P, QKV])
        Wo_raw = sb("Wo_raw", [H * D + 1, C])
        W1hi = sb("W1hi", [P, KB, W1N], F32R)
        W1lo = sb("W1lo", [P, KB, W1N], F32R)
        b1 = sb("b1", [P, C])
        brout = sb("brout", [P, 1])
        guhi = sb("guhi", [P, KB, GUB, P], F32R)
        gulo = sb("gulo", [P, KB, GUB, P], F32R)
        wdhi = sb("wdhi", [P, FB + 1, C], F32R)
        wdlo = sb("wdlo", [P, FB + 1, C], F32R)
        n1col = sb("n1col", [P, KB])
        n2col = sb("n2col", [P, KB])
        bvcol = sb("bvcol", [P, KB])
        modA = sb("modA", [P, C])
        modB = sb("modB", [P, 3, C])
        modc = sb("modc", [P, 2, KB])
        Wqhi = sb("Wqhi", [P, KB, QKV], F32R)
        Wqlo = sb("Wqlo", [P, KB, QKV], F32R)
        bias_q = sb("bias_q", [P, QKV])
        Wo_b = sb("Wo_b", [H * D + 1, C])
        tok = sb("tok", [P, 6, NT * C])
        PT = tok[:, 2:4, :].rearrange("p s (h n) -> p s h n", h=H)
        xbuf, xn, hbuf, hh, x1, obuf = (tok[:, n, :].rearrange("p (t c) -> p t c", t=NT) for n in range(6))
        h2 = xn
        fTh = sb("fTh", [P, TPC, KB, P], F32R)
        fTl = sb("fTl", [P, TPC, KB, P], F32R)
        gTh = sb("gTh", [P, KB, T], F32R)
        gTl = sb("gTl", [P, KB, T], F32R)
        scr = sb("scr", [P, 4, CH])
        qk = scr[:, 0, :].rearrange("p (t h e i) -> p t h e i", t=TPC, h=2 * H, e=2)
        rt = scr[:, 1:3, :].rearrange("p a (b t h i) -> p (a b) t h i", b=2, t=TPC, h=2 * H)
        rot = scr[:, 3, :].rearrange("p (t h d) -> p t h d", t=TPC, h=2 * H)
        sil, fft = scr[:, 0:2, :], scr[:, 2:4, :]
        Qst = sb("Qst", [P, TPC, H, QS])
        Kst = sb("Kst", [P, TPC, H * KSTEP])
        QT = sb("QT", [KR, 2, T], F32R)
        KT = sb("KT", [KR, H, T], F32R)
        V = sb("V", [P, NT, H, 2 * D])
        mx = sb("mx", [P, NT, H])
        mxp = sb("mxp", [P, NT, H, 2])
        mt = sb("mt", [P, NT, H, 2])
        yT = sb("yT", [P, CH])
        rc = sb("rc", [P, TPC, H])
        ytm = sb("ytm", [P, TPC, H * D + 1])
        yT65 = sb("yT65", [H * D + 1, NT, P])
        st = sb("st", [P, NT, 6])
        tick = sb("tick", [P, 1])
        mv1 = sb("mv1", [P, NT, 2])
        mv2 = sb("mv2", [P, NT, 2])
        rstd1 = sb("rstd1", [P, NT])
        rstd2 = sb("rstd2", [P, NT])
        ms = sb("ms", [P, 2, NT])
        rs = sb("rs", [P, 2, NT])
        r_yes = sb("r_yes", [P, NT])
        r_no = sb("r_no", [P, NT])
        sq = sb("sq", [P, 2, C])
        ffhi = sb("ffhi", [P, FB + 1, CH], F32R)
        fflo = sb("fflo", [P, FB, CH], F32R)

        bank = [ctx.enter_context(nc.psum_tensor(f"bank{n}", [P, CH], F32)) for n in range(8)]

        wm_st = tok[:, 1:3, :].rearrange("p a n -> p (a n)")[:, 0:KB * 6 * C].rearrange("p (k n) -> p k n", k=KB)
        wq_st = tok[:, 3, 0:512].rearrange("p (k n) -> p k n", k=KB)
        wk_st = tok[:, 3, 512:640].rearrange("p (k n) -> p k n", k=KB)
        wv_st = tok[:, 3, 640:768].rearrange("p (k n) -> p k n", k=KB)
        bb_st = tok[:, 3, 768:1152]
        fwv_st = tok[:, 3, 1152:1664].rearrange("p (k n) -> p k n", k=KB)
        fwo_st = tok[:, 4, 0:512].rearrange("p (k n) -> p k n", k=KB)
        fwvT = tok[:, 4, 512:1024].rearrange("p (k n) -> p k n", k=KB)
        cT = tok[:, 4, 1024:1032].rearrange("p (k b) -> p k b", k=KB)
        cth = tok[:, 4, 1032:1040].rearrange("p (k b) -> p k b", k=KB)
        csl = tok[:, 4, 1040:1048].rearrange("p (k b) -> p k b", k=KB)
        w1_st = tok[:, 4, 1100:1616].rearrange("p (k n) -> p k n", k=KB)
        wd_st = tok[:, 5, 0:(FB + 1) * C].rearrange("p (k n) -> p k n", k=FB + 1)
        wg_st = tok[:, 1, 0:KB * FF].rearrange("p (k n) -> p k n", k=KB)
        wu_st = tok[:, 2, 0:KB * FF].rearrange("p (k n) -> p k n", k=KB)
        modr = scr[0:B, 0:3, :].rearrange("b a n -> b (a n)")
        gsgn = scr[0:B, 3, :].rearrange("b (m n) -> b m n", m=2)
        gabs = tok[0:B, 5, (FB + 1) * C:(FB + 3) * C].rearrange("b (m n) -> b m n", m=2)

        l_small, l_qkv, l_mod, l_ffn, l_gu, l_wd = (sem(n) for n in (
            "l_small", "l_qkv", "l_mod", "l_ffn", "l_gu", "l_wd"))
        s_const = sem("s_const")
        s_setA, s_setV, s_setP = sem("s_setA"), sem("s_setV"), sem("s_setP")
        s_modw = sem("s_modw")
        s_x, s_modA, s_modB = sem("s_x"), sem("s_modA"), sem("s_modB")
        s_out = sem("s_out")
        N = dict(
            bias_pe=1, biasq=1, wq=1,
            mv1=1, rstd1=1, xn=NT, xT=NT, xhi=NT, xlo=NT,
            qkv=NT, qkvb=NT, rope=NC, sthi=NC, stlo=NC,
            kTp=NT, qTp=NT, kT=NT, qT=NT,
            sc=len(MAX_UNITS), mxd=len(MAX_UNITS), mt=NC, mtp=NC, mrow=NC,
            st=H * len(P_UNITS), p=H * len(P_UNITS), pv=len(P_UNITS),
            yTs=NC, yTp=NC, ytm=NC, ynTp=NC, yn=NC,
            wo=NT, x1=NT, mv2=NT, rstd2=NT, xh=NT, h=NT, hb=NT, ms1=NT, rs1=NT,
            hTp=NT, hhi=NT, hlo=NT, a=NT, r=NT, hh=NT, ms2=NT, rs2=NT, hnr=NT,
            h2=NT, hsel=NT, h2Tp=NT, h2hi=NT, h2lo=NT,
            gu=NC * (FB + 1), up=NC * FB, sil=NC * (FB + 1), fft=NC * (FB + 1), ffhi=NC * (FB + 1),
            fflo=NC * (FB + 1), down=NT, u=NT, o=NT,
            dchain=DVE_CHAIN, pchain=POOL_CHAIN)
        S = {n: sem("s_" + n) for n in N}
        START = {"u": 1}

        BANK, before, last_in = {}, {}, [None] * 8

        def claim(kind, n, where, signal, count):
            BANK[kind, n] = where
            before[kind, n] = last_in[where]
            last_in[where] = (signal, count)

        at_max, at_gu = 0, 0
        for kind, n in STEPS:
            if kind == "weights":
                claim("bias", 0, 7, "biasq", 1)
            elif kind == "xT":
                claim("xT", n, 5 + n % 2, "xlo", n + 1)
            elif kind == "qkv":
                claim("qkv", n, (7, 4)[n % 2], "qkvb", n + 1)
            elif kind == "stackT":
                claim("kTp", n, n % 2, "kT", n + 1)
                claim("qTp", n, 2 + n % 2, "qT", n + 1)
            elif kind == "max":
                claim("max", n, at_max % 2, "mxd", at_max + 1)
                at_max += 1
            elif kind == "maxrow":
                claim("mtp", n, 6, "mrow", n + 1)
            elif kind == "prob":
                for h in range(H):
                    claim("st", (n, h), 2 + h % 2, "p", n * H + h + 1)
            elif kind == "pv" and P_UNITS[n][1] == 0:
                claim("pv", P_UNITS[n][0], 4, "yTs", P_UNITS[n][0] + 1)
            elif kind == "yT":
                claim("yTp", n, 5, "ytm", n + 1)
            elif kind == "ynT":
                claim("ynTp", n, 6, "yn", n + 1)
            elif kind == "wo":
                claim("wo", n, 7, "x1", n + 1)
            elif kind == "hT":
                claim("hTp", n, 5, "hlo", n + 1)
            elif kind == "a":
                claim("a", n, 7, "hh", n + 1)
            elif kind == "h2T":
                claim("h2Tp", n, 6, "h2lo", n + 1)
            elif kind == "gateup":
                claim("gate", n, 2 * (at_gu % 2), "sil" if n[1] < FB else "fft", at_gu + 1)
                if n[1] < FB:
                    claim("upp", n, 2 * (at_gu % 2) + 1, "fft", at_gu + 1)
                at_gu += 1
            elif kind == "down":
                claim("down", n, 4, "u", n + 1)

        kst = Kst[:].rearrange("p t (h n) -> p t h n", h=H)

        def kst_head(h):
            return h * KSTEP - (h % 2) * QS

        def of(kind, n):
            return bank[BANK[kind, n]]

        def max_index(c, n):
            return sum(len(m) for m in MAX_OF_CHUNK[:c]) + n

        def flat(ap):
            return ap.rearrange("p k n -> p (k n)")

        def by_block(ap):
            return ap.rearrange("p (k n) -> p k n", k=KB)

        block = ctx.enter_context(nc.Block())

        @block.sync
        def _(sp):
            def load_x(b):
                sp.dma_start(xbuf, x[bass.ds(b, 1), :, :].rearrange("o (t p) c -> p (o t) c", p=P)).then_inc(s_x, 16)

            load_x(0)
            for k in range(KB):
                sp.dma_start(cT[:, k, :], c_in[:, k * P:(k + 1) * P].rearrange("b p -> p b")).then_inc(l_mod, 16)
            sp.dma_start(wm_st, wmod.rearrange("(k p) n -> p k n", p=P)).then_inc(l_mod, 16)
            sp.dma_start(wq_st, Wq.rearrange("(k p) n -> p k n", p=P)).then_inc(l_qkv, 16)
            sp.dma_start(wk_st, Wk.rearrange("(k p) n -> p k n", p=P)).then_inc(l_qkv, 16)
            sp.dma_start(wv_st, Wv.rearrange("(k p) n -> p k n", p=P)).then_inc(l_qkv, 16)
            sp.dma_start(bb_st[:, 0:C], bq.partition_broadcast(P)).then_inc(l_qkv, 16)
            sp.dma_start(bb_st[:, C:C + 64], bk.partition_broadcast(P)).then_inc(l_qkv, 16)
            sp.dma_start(bb_st[:, C + 64:C + 128], bv.partition_broadcast(P)).then_inc(l_qkv, 16)
            sp.dma_start(cos_t[:], rope_cos).then_inc(l_small, 16)
            sp.dma_start(sin_t[:], rope_sin).then_inc(l_small, 16)
            sp.dma_start(Wo_raw[0:H * D, :], Wo).then_inc(l_small, 16)
            sp.dma_start(Wo_raw[H * D:H * D + 1, :], bo.unsqueeze(0)).then_inc(l_small, 16)
            sp.dma_start(brout[:], b_router.partition_broadcast(P)).then_inc(l_small, 16)
            sp.dma_start(fwv_st, f_wv.rearrange("(k p) n -> p k n", p=P)).then_inc(l_ffn, 16)
            sp.dma_start(fwo_st, f_wo.rearrange("(k p) n -> p k n", p=P)).then_inc(l_ffn, 16)
            sp.dma_start(n1col[:], n1.rearrange("(k p) -> p k", p=P)).then_inc(l_ffn, 16)
            sp.dma_start(n2col[:], n2.rearrange("(k p) -> p k", p=P)).then_inc(l_ffn, 16)
            sp.dma_start(bvcol[:], f_bv.rearrange("(k p) -> p k", p=P)).then_inc(l_ffn, 16)
            sp.dma_start(w1_st[:, :, C], w_router.rearrange("(k p) -> p k", p=P)).then_inc(l_ffn, 16)
            sp.dma_start(wd_st[:, 0:FB, :], w_down[0:FB * P, :].rearrange("(k p) n -> p k n", p=P)).then_inc(l_wd, 16)
            sp.dma_start(wd_st[0:FR, FB, :], w_down[FB * P:FF, :]).then_inc(l_wd, 16)
            sp.dma_start(wd_st[FR:P, FB, :], w_down[FB * P:FF, :]).then_inc(l_wd, 16)
            sp.wait_ge(s_setP, 1)
            sp.dma_start(wg_st, w_gate.rearrange("(k p) n -> p k n", p=P)).then_inc(l_gu, 16)
            sp.dma_start(wu_st, w_up.rearrange("(k p) n -> p k n", p=P)).then_inc(l_gu, 16)
            sp.wait_ge(s_setV, V_MOD)
            sp.dma_start(mod_dram, modr).then_inc(s_modw, 16)
            sp.wait_ge(s_modw, 16)
            sp.sem_inc(s_out, 1)

            def load_modA(b):
                for v in range(2):
                    sp.dma_start(modc[:, v, :], mod_dram[bass.ds(b, 1), v * C:(v + 1) * C].rearrange(
                        "o (k p) -> p (o k)", p=P)).then_inc(s_modA, 16)
                sp.dma_start(modA[:], mod_dram[bass.ds(b, 1), 2 * C:3 * C].rearrange("o n -> (o n)"
                             ).partition_broadcast(P)).then_inc(s_modA, 16)

            def load_modB(b):
                sp.dma_start(modB[:].rearrange("p v n -> p (v n)"), mod_dram[bass.ds(b, 1), 3 * C:6 * C].rearrange(
                    "o n -> (o n)").partition_broadcast(P)).then_inc(s_modB, 16)

            def store(b):
                for c in range(NC):
                    sp.wait_ge(S["o"], b * N["o"] + (c + 1) * TPC)
                    sp.dma_start(out[bass.ds(b, 1), c * CH:(c + 1) * CH, :].rearrange("o (t p) c -> p (o t) c", p=P),
                                 obuf[:, c * TPC:(c + 1) * TPC, :]).then_inc(s_out, 16)

            load_modA(0)
            load_modB(0)
            with sp.Fori(0, B - 1) as b:
                sp.wait_ge(S["biasq"], b * N["biasq"] + 1)
                load_modA(b + 1)
                sp.wait_ge(S["x1"], b * N["x1"] + NT)
                load_x(b + 1)
                store(b)
                load_modB(b + 1)
            store(B - 1)
            sp.wait_ge(s_out, 16 * NC * B + 1)

        @block.gpsimd
        def _(pool):
            pool.memset(ident[:], 0.0)
            pool.memset(mask_qk[:], 0.0)
            pool.memset(mask_kq[:], 0.0)
            pool.memset(expo[:], -0.5)
            pool.memset(eps_ln[:], LN_EPS)
            pool.memset(eps_rms[:], RMS_EPS)
            pool.memset(V[:], 0.0)
            pool.memset(Kst[:], 0.0)
            pool.memset(ytm[:], 1.0).then_inc(s_const, 1)
            pool.wait_ge(s_const, 1)
            pool.affine_select(out=ident[:], in_=ident[:], compare_op=ALU.not_equal, fill=1.0, base=0,
                               pattern=[[-1, P]], channel_multiplier=1)
            pool.affine_select(out=mask_qk[:], in_=mask_qk[:], compare_op=ALU.is_ge, fill=NEG, base=0,
                               pattern=[[-1, P]], channel_multiplier=1)
            pool.affine_select(out=mask_kq[:], in_=mask_kq[:], compare_op=ALU.is_ge, fill=NEG, base=0,
                               pattern=[[1, P]], channel_multiplier=-1)
            for h in range(H):
                at = kst_head(h) + QP + 2 * h
                pool.memset(Kst[:, :, at:at + 2], 1.0)
            pool.memset(V[:, :, :, D:D + 1], 1.0).then_inc(s_const, 1)
            pool.wait_ge(s_const, 2)
            pool.tensor_copy(ident_b[:], ident[:]).then_inc(s_const, 1)

            chain = [0]
            with pool.Fori(0, B) as b:
                def wait(name, k):
                    pool.wait_ge(S[name], b * N[name] + k + START.get(name, 0))

                def then(i):
                    i.then_inc(S["pchain"], 1)
                    chain[0] += 1
                    wait("pchain", chain[0])

                def rsqrt(dst, src, eps, done):
                    then(pool.tensor_tensor(dst, src, eps, ALU.add))
                    pool.tensor_tensor(dst, dst, expo[:, 0:dst.shape[1]], ALU.pow).then_inc(done, 1)

                for kind, n in STEPS:
                    if kind == "norm1":
                        wait("mv1", 1)
                        rsqrt(rstd1[:], mv1[:, :, 1], eps_ln[:], S["rstd1"])
                    elif kind == "wo":
                        wait("mv2", n + 1)
                        rsqrt(rstd2[:, n:n + 1], mv2[:, n, 1:2], eps_ln[:, 0:1], S["rstd2"])
                    elif kind == "norm2":
                        if n == 0:
                            pool.wait_ge(s_modB, 16 * b + 16)
                        wait("xh", n + 1)
                        then(pool.tensor_tensor(hbuf[:, n, :], hbuf[:, n, :], modB[:, 1, :], ALU.mult))
                        pool.tensor_tensor(hbuf[:, n, :], hbuf[:, n, :], modB[:, 0, :], ALU.add).then_inc(S["h"], 1)
                        wait("h", n + 1)
                        pool.tensor_tensor(hh[:, n, :], hbuf[:, n, :], b1[:], ALU.add).then_inc(S["hb"], 1)
                        wait("ms1", n + 1)
                        rsqrt(rs[:, 0, n:n + 1], ms[:, 0, n:n + 1], eps_rms[:, 0:1], S["rs1"])
                    elif kind == "a":
                        wait("ms2", n + 1)
                        rsqrt(rs[:, 1, n:n + 1], ms[:, 1, n:n + 1], eps_rms[:, 0:1], S["rs2"])
                    elif kind == "down":
                        wait("u", n + 1)
                        then(pool.tensor_tensor(obuf[:, n, :], obuf[:, n, :], modB[:, 2, :], ALU.mult))
                        pool.tensor_tensor(obuf[:, n, :], obuf[:, n, :], x1[:, n, :], ALU.add).then_inc(S["o"], 1)
            assert chain[0] == POOL_CHAIN, chain[0]

        @block.tensor
        def _(pe):
            pe.wait_ge(s_setV, V_CSL)
            for n in range(3):
                for k in range(KB):
                    i = pe.matmul(bank[n][0:B, :], csl[:, k, :], wm_st[:, k, n * CH:(n + 1) * CH],
                                  start=(k == 0), stop=(k == KB - 1))
            i.then_inc(s_setP, 1)
            pe.wait_ge(l_ffn, 96)
            pe.wait_ge(s_const, 3)
            for d in range(KB):
                for k in range(KB):
                    i = pe.transpose(bank[3][:, (d * KB + k) * P:(d * KB + k + 1) * P],
                                     fwv_st[:, k, d * P:(d + 1) * P], ident[:])
            i.then_inc(s_setP, 1)
            pe.wait_ge(s_setV, V_FWVT)
            for k in range(KB):
                for d in range(KB):
                    pe.matmul(bank[4 + k][:, 0:C], fwvT[:, d, k * P:(k + 1) * P], fwo_st[:, d, :],
                              start=(d == 0), stop=(d == KB - 1))
            for d in range(KB):
                i = pe.matmul(bank[6][:, 0:C], bvcol[:, d:d + 1].to_broadcast([P, P]), fwo_st[:, d, :],
                              start=(d == 0), stop=(d == KB - 1))
            i.then_inc(s_setP, 1)

            def three_pass(o, hi, lo, whi, wlo, first, last):
                pe.matmul(o, hi, whi, start=first, stop=False)
                pe.matmul(o, hi, wlo, start=False, stop=False)
                return pe.matmul(o, lo, whi, start=False, stop=last)

            with pe.Fori(0, B) as b:
                def wait(name, k):
                    pe.wait_ge(S[name], b * N[name] + k + START.get(name, 0))

                def take(kind, n):
                    if before[kind, n] is not None:
                        wait(*before[kind, n])
                    return of(kind, n)

                wait("u", 0)
                for kind, n in STEPS:
                    if kind == "weights":
                        pe.wait_ge(s_modA, 48 * b + 48)
                        o = take("bias", 0)
                        for k in range(KB):
                            i = pe.matmul(o[:, 0:QKV], modc[:, 0, k:k + 1].to_broadcast([P, P]), Wqkv[:, k, :],
                                          start=(k == 0), stop=(k == KB - 1))
                        i.then_inc(S["bias_pe"], 1)
                    elif kind == "xT":
                        wait("xn", n + 1)
                        o = take("xT", n)
                        for k in range(KB):
                            i = pe.transpose(o[:, k * P:(k + 1) * P], xn[:, n, k * P:(k + 1) * P], ident[:])
                        i.then_inc(S["xT"], 1)
                    elif kind == "qkv":
                        if n == 0:
                            wait("wq", 1)
                        wait("xlo", n + 1)
                        o = take("qkv", n)
                        for k in range(KB):
                            i = three_pass(o[:, 0:QKV], fTh[:, n % TPC, k, :], fTl[:, n % TPC, k, :], Wqhi[:, k, :], Wqlo[:, k, :],
                                           k == 0, k == KB - 1)
                        i.then_inc(S["qkv"], 1)
                    elif kind == "stackT":
                        if n % TPC == 0:
                            wait("sthi", n // TPC + 1)
                            wait("stlo", n // TPC + 1)
                        o = take("kTp", n)
                        for h in range(H):
                            at = kst_head(h)
                            i = pe.transpose(o[0:KR, h * P:(h + 1) * P], Kst[:, n % TPC, at:at + KR], ident[:])
                        i.then_inc(S["kTp"], 1)
                        o = take("qTp", n)
                        for q in range(2):
                            i = pe.transpose(o[0:QP, q * P:(q + 1) * P], Qst[:, n % TPC, 2 * q:2 * q + 2, :].rearrange(
                                "p h d -> p (h d)"), ident[:])
                        i.then_inc(S["qTp"], 1)
                    elif kind == "max":
                        qt, k0, kn, h0, hn = MAX_OF_CHUNK[n[0]][n[1]]
                        wait("kT", qt + 1)
                        wait("qT", qt + 1)
                        o = take("max", n)
                        diag = k0 + kn == (qt + 1) * P
                        for h in range(h0, h0 + hn):
                            col = (h - h0) * kn
                            i = pe.matmul(o[:, col:col + kn], QT[0:QP, h // 2, qt * P:(qt + 1) * P],
                                          KT[0:QP, h, k0:k0 + kn], start=True, stop=not diag)
                            if diag:
                                i = pe.matmul(o[:, col + kn - P:col + kn], ident_b[:], mask_qk[:],
                                              start=False, stop=True)
                        i.then_inc(S["sc"], 1)
                    elif kind == "maxrow":
                        wait("mt", n + 1)
                        o = take("mtp", n)
                        for t in range(TPC):
                            i = pe.transpose(o[0:2 * H, t * P:(t + 1) * P],
                                             mt[:, n * TPC + t, :, :].rearrange("p h e -> p (h e)"), ident[:])
                        i.then_inc(S["mtp"], 1)
                    elif kind == "prob":
                        c, j, q0 = P_UNITS[n]
                        if j == 0:
                            wait("mrow", c + 1)
                        for h in range(H):
                            o = take("st", (n, h))
                            diag = j >= c * TPC
                            i = pe.matmul(o[:, 0:CH - q0], KT[:, h, j * P:(j + 1) * P],
                                          QT[:, h // 2, c * CH + q0:(c + 1) * CH], start=True, stop=not diag)
                            if diag:
                                i = pe.matmul(o[:, 0:P], ident_b[:], mask_kq[:], start=False, stop=True)
                            i.then_inc(S["st"], 1)
                    elif kind == "pv":
                        c, j, q0 = P_UNITS[n]
                        wait("p", H * (n + 1))
                        o = take("pv", c) if j == 0 else of("pv", c)
                        for h in range(H):
                            i = pe.matmul(o[h * 2 * D:(h + 1) * 2 * D, q0:CH], V[:, j, h, :],
                                          PT[:, n % 2, h, 0:CH - q0], start=(j == 0), stop=(q0 == CH - P),
                                          skip_group_check=True)
                        i.then_inc(S["pv"], 1)
                    elif kind == "yT":
                        wait("yTs", n + 1)
                        o = take("yTp", n)
                        for t in range(TPC):
                            i = pe.transpose(o[:, t * P:(t + 1) * P], yT[:, t * P:(t + 1) * P], ident[:])
                        i.then_inc(S["yTp"], 1)
                    elif kind == "ynT":
                        wait("ytm", n + 1)
                        o = take("ynTp", n)
                        for t in range(TPC):
                            i = pe.transpose(o[0:H * D + 1, t * P:(t + 1) * P], ytm[:, t, :], ident[:])
                        i.then_inc(S["ynTp"], 1)
                    elif kind == "wo":
                        wait("yn", n // TPC + 1)
                        o = take("wo", n)
                        pe.matmul(o[:, 0:C], yT65[:, n, :], Wo_b[:], start=True, stop=True).then_inc(S["wo"], 1)
                    elif kind == "hT":
                        wait("h", n + 1)
                        o = take("hTp", n)
                        for k in range(KB):
                            i = pe.transpose(o[:, k * P:(k + 1) * P], hbuf[:, n, k * P:(k + 1) * P], ident[:])
                        i.then_inc(S["hTp"], 1)
                    elif kind == "a":
                        wait("hlo", n + 1)
                        o = take("a", n)
                        for k in range(KB):
                            i = three_pass(o[:, 0:W1N], fTh[:, n % TPC, k, :], fTl[:, n % TPC, k, :], W1hi[:, k, :], W1lo[:, k, :],
                                           k == 0, k == KB - 1)
                        i.then_inc(S["a"], 1)
                    elif kind == "h2T":
                        wait("h2", n + 1)
                        o = take("h2Tp", n)
                        for k in range(KB):
                            i = pe.transpose(o[:, k * P:(k + 1) * P], h2[:, n, k * P:(k + 1) * P], ident[:])
                        i.then_inc(S["h2Tp"], 1)
                    elif kind == "gateup":
                        c, f = n
                        if f == 0:
                            wait("h2lo", (c + 1) * TPC)
                        cols = slice(c * CH, (c + 1) * CH)
                        for what, blk in ((("gate", f), ("upp", FB + f)) if f < FB else (("gate", 2 * FB),)):
                            o = take(what, n)
                            for k in range(KB):
                                pe.matmul(o[:], guhi[:, k, blk, :], gTh[:, k, cols], start=(k == 0), stop=False)
                                pe.matmul(o[:], guhi[:, k, blk, :], gTl[:, k, cols], start=False, stop=False)
                                i = pe.matmul(o[:], gulo[:, k, blk, :], gTh[:, k, cols], start=False,
                                              stop=(k == KB - 1))
                            i.then_inc(S["gu" if what == "gate" else "up"], 1)
                    elif kind == "down":
                        c, t = n // TPC, n % TPC
                        if t == 0:
                            wait("fflo", (c + 1) * (FB + 1))
                        o = take("down", n)[:, 0:C]
                        cols = slice(t * P, (t + 1) * P)
                        for f in range(FB):
                            three_pass(o, ffhi[:, f, cols], fflo[:, f, cols], wdhi[:, f, :], wdlo[:, f, :],
                                       f == 0, False)
                        pe.matmul(o, ffhi[:, FB, cols], wdhi[:, FB, :], start=False, stop=False)
                        pe.matmul(o, ffhi[:, FB, cols], wdlo[:, FB, :], start=False, stop=True
                                  ).then_inc(S["down"], 1)

        @block.scalar
        def _(act):
            act.wait_ge(l_mod, 48)
            act.activation(cth, cT, ACT.Tanh, scale=0.5).then_inc(s_setA, 1)
            with act.Fori(0, B) as b:
                def wait(name, k):
                    act.wait_ge(S[name], b * N[name] + k + START.get(name, 0))

                for kind, n in STEPS:
                    if kind == "xT":
                        wait("xT", n + 1)
                        if n >= TPC:
                            wait("qkv", n - TPC + 1)
                        act.activation(flat(fTh[:, n % TPC, :, :]), of("xT", n)[:, 0:C], ACT.Copy).then_inc(S["xhi"], 1)
                    elif kind == "rope":
                        wait("rope", n + 1)
                        if n > 0:
                            wait("qTp", n * TPC)
                        for at in (0, D):
                            act.activation(Qst[:, :, :, at:at + D].bitcast(F32R), rot[:, :, 0:H, :], ACT.Copy)
                        for at in (0, 2 * D):
                            i = act.activation(kst[:, :, :, at:at + D].bitcast(F32R), rot[:, :, H:2 * H, :], ACT.Copy)
                        i.then_inc(S["sthi"], 1)
                    elif kind == "stackT":
                        wait("kTp", n + 1)
                        act.activation(KT[:, :, n * P:(n + 1) * P],
                                       of("kTp", n)[0:KR, :].rearrange("p (h n) -> p h n", h=H), ACT.Copy
                                       ).then_inc(S["kT"], 1)
                    elif kind == "maxrow":
                        wait("mtp", n + 1)
                        for q in range(2):
                            i = act.activation(QT[QP:KR, q, n * CH:(n + 1) * CH], of("mtp", n)[0:2 * H, :], ACT.Copy)
                        i.then_inc(S["mrow"], 1)
                    elif kind == "prob":
                        c, j, q0 = P_UNITS[n]
                        if n >= 2:
                            wait("pv", n - 1)
                        for h in range(H):
                            wait("st", n * H + h + 1)
                            act.activation(PT[:, n % 2, h, 0:CH - q0], of("st", (n, h))[:, 0:CH - q0], ACT.Exp,
                                           scale=float(D) ** -0.5).then_inc(S["p"], 1)
                    elif kind == "ycopy":
                        wait("pv", [m + 1 for m, u in enumerate(P_UNITS) if u[0] == n][-1])
                        if n > 0:
                            wait("yTp", n)
                        act.activation(yT[:], of("pv", n)[:], ACT.Copy).then_inc(S["yTs"], 1)
                    elif kind == "ynT":
                        wait("ynTp", n + 1)
                        act.activation(yT65[:, n * TPC:(n + 1) * TPC, :].rearrange("p t n -> p (t n)"),
                                       of("ynTp", n)[0:H * D + 1, :], ACT.Copy).then_inc(S["yn"], 1)
                    elif kind == "norm2":
                        wait("h", n + 1)
                        if n > 0:
                            wait("ms1", n)
                        act.activation(sq[:, 0, :], hbuf[:, n, :], ACT.Square, scale=float(C) ** -0.5,
                                       accum_out=ms[:, 0, n:n + 1]).then_inc(S["ms1"], 1)
                    elif kind == "hT":
                        wait("hTp", n + 1)
                        if n >= TPC:
                            wait("a", n - TPC + 1)
                        act.activation(flat(fTh[:, n % TPC, :, :]), of("hTp", n)[:, 0:C], ACT.Copy).then_inc(S["hhi"], 1)
                    elif kind == "a":
                        wait("hh", n + 1)
                        if n > 0:
                            wait("ms2", n)
                        act.activation(sq[:, 1, :], hh[:, n, :], ACT.Square, scale=float(C) ** -0.5,
                                       accum_out=ms[:, 1, n:n + 1]).then_inc(S["ms2"], 1)
                        act.activation(hbuf[:, n, :], hbuf[:, n, :], ACT.Copy, scale=r_no[:, n:n + 1]
                                       ).then_inc(S["hnr"], 1)
                    elif kind == "h2T":
                        wait("h2Tp", n + 1)
                        act.activation(gTh[:, :, n * P:(n + 1) * P], by_block(of("h2Tp", n)[:, 0:C]), ACT.Copy
                                       ).then_inc(S["h2hi"], 1)
                    elif kind == "gateup":
                        c, f = n
                        m = c * (FB + 1) + f
                        wait("gu", m + 1)
                        if m >= 2:
                            wait("fft", m - 1)
                        if f < FB:
                            act.activation(sil[:, m % 2, :], of("gate", n)[:], ACT.Silu).then_inc(S["sil"], 1)
                        else:
                            act.activation(sil[FR:P, m % 2, :], of("gate", n)[0:FR, :], ACT.Silu
                                           ).then_inc(S["sil"], 1)
                        wait("fft", m + 1)
                        if f == 0 and c > 0:
                            wait("down", c * TPC)
                        rows = P if f < FB else FR
                        act.activation(ffhi[0:rows, f, :], fft[0:rows, m % 2, :], ACT.Copy).then_inc(S["ffhi"], 1)

        @block.vector
        def _(dve):
            done = [0]

            def setup(i):
                i.then_inc(s_setV, 1)
                done[0] += 1
                return done[0]

            def setup_then(i):
                k = setup(i)
                dve.wait_ge(s_setV, k)

            dve.wait_ge(s_setA, 1)
            setup_then(dve.scalar_tensor_tensor(csl, cth, 1.0, cT, ALU.add, ALU.mult))
            assert setup(dve.tensor_scalar(csl, csl, 0.5, None, ALU.mult)) == V_CSL
            dve.wait_ge(l_qkv, 96)
            groups = [(wq_st[:, k, :], wk_st[:, k, :], wv_st[:, k, :], Wqkv[:, k, :]) for k in range(KB)]
            groups += [(bb_st[:, 0:C], bb_st[:, C:C + H * D], bb_st[:, C + H * D:C + 2 * H * D], bqkv[:])]
            for wq, wk, wv, w in groups:
                for e in range(2):
                    dve.tensor_reduce(w[:, 0:H * D].rearrange("p (h e i) -> p e h i", h=H, e=2)[:, e],
                                      wq.rearrange("p (h g i e) -> p e h i g", h=H, g=G, e=2)[:, e], AX.X, ALU.add)
                    dve.tensor_copy(w[:, H * D:2 * H * D].rearrange("p (h e i) -> p e h i", h=H, e=2)[:, e],
                                    wk.rearrange("p (h i e) -> p e h i", h=H, e=2)[:, e])
                i = dve.tensor_copy(w[:, 2 * H * D:QKV], wv)
            setup(i)
            dve.wait_ge(s_setP, 1)
            for n in range(3):
                i = dve.tensor_copy(modr[:, n * CH:(n + 1) * CH], bank[n][0:B, :])
            setup_then(i)
            rows = modr.rearrange("b (m v n) -> b m v n", m=2, v=3)
            dve.tensor_scalar(rows[:, :, 1, :], rows[:, :, 1, :], 1.0, None, ALU.add)
            setup_then(dve.tensor_scalar(gsgn, rows[:, :, 2, :], 0.0, 2.0, ALU.is_ge, ALU.mult))
            setup_then(dve.scalar_tensor_tensor(gabs, gsgn, -1.0, rows[:, :, 2, :], ALU.add, ALU.mult))
            setup_then(dve.tensor_scalar(gabs, gabs, 0.25, None, ALU.max))
            assert setup(dve.scalar_tensor_tensor(rows[:, :, 2, :], gsgn, -1.0, gabs, ALU.add, ALU.mult)
                         ) == V_MOD
            dve.wait_ge(s_setP, 2)
            assert setup(dve.tensor_copy(flat(fwvT), bank[3][:])) == V_FWVT
            dve.wait_ge(s_setP, 3)
            for k in range(KB):
                dve.tensor_scalar(w1_st[:, k, 0:C], bank[4 + k][:, 0:C], n1col[:, k:k + 1], None, ALU.mult)
                dve.memset(w1_st[:, k, C + 1:C + 2], 0.0)
            setup_then(dve.tensor_copy(b1[:], bank[6][:, 0:C]))
            setup_then(dve.tensor_copy(W1hi[:], w1_st))
            dve.tensor_tensor(W1lo[:], w1_st, W1hi[:].bitcast(F32), ALU.subtract)
            dve.wait_ge(l_gu, 32)
            pieces = []
            for k in range(KB):
                for j, w in enumerate((wg_st, wu_st)):
                    pieces.append((w[:, k, 0:FB * P], k, slice(j * FB, (j + 1) * FB), slice(0, P)))
                    pieces.append((w[:, k, FB * P:FF], k, slice(2 * FB, GUB), slice(j * FR, (j + 1) * FR)))
            for src, k, blk, cols in pieces:
                hi = guhi[:, k, blk, cols]
                i = dve.tensor_scalar(hi, src.rearrange("p (f n) -> p f n", n=hi.shape[2]), n2col[:, k:k + 1], None,
                                      ALU.mult)
            setup_then(i)
            for src, k, blk, cols in pieces:
                hi = guhi[:, k, blk, cols]
                dve.scalar_tensor_tensor(gulo[:, k, blk, cols], src.rearrange("p (f n) -> p f n", n=hi.shape[2]),
                                         n2col[:, k:k + 1], hi.bitcast(F32), ALU.mult, ALU.subtract)
            dve.wait_ge(l_wd, 48)
            setup_then(dve.tensor_copy(wdhi[:], wd_st))
            setup_then(dve.tensor_tensor(wdlo[:], wd_st, wdhi[:].bitcast(F32), ALU.subtract))
            dve.wait_ge(l_small, 80)
            dve.wait_ge(s_const, 3)
            dve.tensor_copy(tick[:], brout[:]).then_inc(S["u"], 1)

            chain = [0]
            with dve.Fori(0, B) as b:
                def wait(name, k):
                    dve.wait_ge(S[name], b * N[name] + k + START.get(name, 0))

                def then(i):
                    i.then_inc(S["dchain"], 1)
                    chain[0] += 1
                    wait("dchain", chain[0])


                for kind, n in STEPS:
                    if kind == "weights":
                        dve.wait_ge(s_modA, 48 * b + 48)
                        for k in range(KB):
                            i = dve.tensor_scalar(Wqhi[:, k, :], Wqkv[:, k, :], modc[:, 1, k:k + 1], None, ALU.mult)
                        then(i)
                        for k in range(KB):
                            i = dve.scalar_tensor_tensor(Wqlo[:, k, :], Wqkv[:, k, :], modc[:, 1, k:k + 1],
                                                         Wqhi[:, k, :].bitcast(F32), ALU.mult, ALU.subtract)
                        i.then_inc(S["wq"], 1)
                        dve.tensor_tensor(Wo_b[:], Wo_raw[:], modA[0:H * D + 1, :], ALU.mult)
                        wait("bias_pe", 1)
                        dve.tensor_tensor(bias_q[:], of("bias", 0)[:, 0:QKV], bqkv[:], ALU.add
                                          ).then_inc(S["biasq"], 1)
                    elif kind == "norm1":
                        dve.wait_ge(s_x, 16 * b + 16)
                        for t in range(NT):
                            i = dve.bn_stats(st[:, t, :], xbuf[:, t, :])
                        then(i)
                        dve.memset(tick[:], 0.0)
                        for t in range(NT):
                            i = dve.bn_aggr(mv1[:, t, :], st[:, t, :])
                        i.then_inc(S["mv1"], 1)
                        wait("rstd1", 1)
                        for t in range(NT):
                            dve.tensor_scalar(xn[:, t, :], xbuf[:, t, :], mv1[:, t, 0:1], rstd1[:, t:t + 1],
                                              ALU.subtract, ALU.mult).then_inc(S["xn"], 1)
                    elif kind == "xT":
                        wait("xhi", n + 1)
                        dve.tensor_tensor(flat(fTl[:, n % TPC, :, :]), of("xT", n)[:, 0:C],
                                          flat(fTh[:, n % TPC, :, :]).bitcast(F32), ALU.subtract).then_inc(S["xlo"], 1)
                    elif kind == "qkv":
                        wait("qkv", n + 1)
                        o = of("qkv", n)
                        dve.tensor_tensor(qk[:, n % TPC, :, :, :].rearrange("p h e i -> p (h e i)"),
                                          o[:, 0:2 * H * D], bias_q[:, 0:2 * H * D], ALU.add)
                        dve.tensor_tensor(V[:, n, :, 0:D], o[:, 2 * H * D:QKV].rearrange("p (h d) -> p h d", h=H),
                                          bias_q[:, 2 * H * D:QKV].rearrange("p (h d) -> p h d", h=H), ALU.add
                                          ).then_inc(S["qkvb"], 1)
                    elif kind == "rope":
                        wait("qkvb", (n + 1) * TPC)
                        if n > 0:
                            wait("sthi", n)
                            wait("qTp", n * TPC)
                        ts = slice(n * TPC, (n + 1) * TPC)
                        cs = cos_t[:, ts, :].unsqueeze(2).to_broadcast([P, TPC, 2 * H, HALF])
                        sn = sin_t[:, ts, :].unsqueeze(2).to_broadcast([P, TPC, 2 * H, HALF])
                        ev, od = qk[:, :, :, 0, :], qk[:, :, :, 1, :]
                        for m, (u, v) in enumerate(((ev, cs), (od, sn), (ev, sn), (od, cs))):
                            i = dve.tensor_tensor(rt[:, m], u, v, ALU.mult)
                        then(i)
                        dve.tensor_tensor(rot[:, :, :, 0:HALF], rt[:, 0], rt[:, 1], ALU.subtract)
                        dve.tensor_tensor(rot[:, :, :, HALF:D], rt[:, 2], rt[:, 3], ALU.add).then_inc(S["rope"], 1)
                        wait("sthi", n + 1)
                        dve.tensor_tensor(Qst[:, :, :, 2 * D:3 * D].bitcast(F32R), rot[:, :, 0:H, :],
                                          Qst[:, :, :, 0:D], ALU.subtract)
                        dve.tensor_tensor(kst[:, :, :, D:2 * D].bitcast(F32R), rot[:, :, H:2 * H, :],
                                          kst[:, :, :, 0:D], ALU.subtract).then_inc(S["stlo"], 1)
                    elif kind == "stackT":
                        wait("qTp", n + 1)
                        dve.tensor_copy(QT[0:QP, :, n * P:(n + 1) * P],
                                        by_block(of("qTp", n)[0:QP, 0:2 * P])).then_inc(S["qT"], 1)
                    elif kind == "max":
                        qt, k0, kn, h0, hn = MAX_OF_CHUNK[n[0]][n[1]]
                        wait("sc", max_index(*n) + 1)
                        dst = mx[:, qt, h0:h0 + hn] if qt < TPC else mxp[:, qt, h0:h0 + hn, k0 // CH]
                        dve.tensor_reduce(dst, of("max", n)[:, 0:hn * kn].rearrange("p (h k) -> p h k", h=hn), AX.X,
                                          ALU.max).then_inc(S["mxd"], 1)
                    elif kind == "maxrow":
                        ts = slice(n * TPC, (n + 1) * TPC)
                        wait("mxd", max_index(n, len(MAX_OF_CHUNK[n])))
                        if n > 0:
                            then(dve.tensor_reduce(mx[:, ts, :], mxp[:, ts, :, :], AX.X, ALU.max))
                        then(dve.tensor_scalar(mt[:, ts, :, 0].bitcast(F32R), mx[:, ts, :], -1.0, None, ALU.mult))
                        dve.scalar_tensor_tensor(mt[:, ts, :, 1].bitcast(F32R), mx[:, ts, :], -1.0,
                                                 mt[:, ts, :, 0], ALU.mult, ALU.subtract).then_inc(S["mt"], 1)
                    elif kind == "yT":
                        wait("yTp", n + 1)
                        if n > 0:
                            wait("ynTp", n)
                        o = of("yTp", n)[:].rearrange("p (t h d) -> p t h d", t=TPC, h=H)
                        then(dve.reciprocal(rc[:], o[:, :, :, D]))
                        dve.tensor_tensor(ytm[:, :, 0:H * D].rearrange("p t (h d) -> p t h d", h=H), o[:, :, :, 0:D],
                                          rc[:].unsqueeze(3).to_broadcast([P, TPC, H, D]), ALU.mult
                                          ).then_inc(S["ytm"], 1)
                    elif kind == "wo":
                        wait("wo", n + 1)
                        dve.tensor_tensor(x1[:, n, :], of("wo", n)[:, 0:C], xbuf[:, n, :], ALU.add
                                          ).then_inc(S["x1"], 1)
                        wait("x1", n + 1)
                        then(dve.bn_stats(st[:, n, :], x1[:, n, :]))
                        dve.memset(tick[:], 0.0)
                        dve.bn_aggr(mv2[:, n, :], st[:, n, :]).then_inc(S["mv2"], 1)
                    elif kind == "norm2":
                        wait("rstd2", n + 1)
                        dve.tensor_scalar(hbuf[:, n, :], x1[:, n, :], mv2[:, n, 0:1], rstd2[:, n:n + 1],
                                          ALU.subtract, ALU.mult).then_inc(S["xh"], 1)
                    elif kind == "hT":
                        wait("hhi", n + 1)
                        dve.tensor_tensor(flat(fTl[:, n % TPC, :, :]), of("hTp", n)[:, 0:C],
                                          flat(fTh[:, n % TPC, :, :]).bitcast(F32), ALU.subtract).then_inc(S["hlo"], 1)
                    elif kind == "a":
                        wait("a", n + 1)
                        wait("rs1", n + 1)
                        wait("hb", n + 1)
                        o = of("a", n)
                        dve.tensor_scalar(r_no[:, n:n + 1], o[:, C:C + 1], brout[:], 0.0, ALU.add, ALU.is_le)
                        dve.tensor_scalar(r_yes[:, n:n + 1], o[:, C:C + 1], brout[:], 0.0, ALU.add, ALU.is_gt)
                        dve.scalar_tensor_tensor(hh[:, n, :], o[:, 0:C], rs[:, 0, n:n + 1], hh[:, n, :],
                                                 ALU.mult, ALU.add).then_inc(S["hh"], 1)
                    elif kind == "h2":
                        wait("rs2", n + 1)
                        dve.tensor_scalar(h2[:, n, :], hh[:, n, :], rs[:, 1, n:n + 1], None, ALU.mult
                                          ).then_inc(S["h2"], 1)
                        wait("hnr", n + 1)
                        dve.scalar_tensor_tensor(hbuf[:, n, :], hh[:, n, :], r_yes[:, n:n + 1], hbuf[:, n, :],
                                                 ALU.mult, ALU.add).then_inc(S["hsel"], 1)
                    elif kind == "h2T":
                        wait("h2hi", n + 1)
                        cols = slice(n * P, (n + 1) * P)
                        dve.tensor_tensor(gTl[:, :, cols], by_block(of("h2Tp", n)[:, 0:C]),
                                          gTh[:, :, cols].bitcast(F32), ALU.subtract).then_inc(S["h2lo"], 1)
                    elif kind == "gateup":
                        c, f = n
                        m = c * (FB + 1) + f
                        wait("sil", m + 1)
                        if m >= 2:
                            wait("ffhi", m - 1)
                        if f < FB:
                            wait("up", c * FB + f + 1)
                            i = dve.tensor_tensor(fft[:, m % 2, :], sil[:, m % 2, :], of("upp", n)[:], ALU.mult)
                        else:
                            i = dve.tensor_tensor(fft[0:FR, m % 2, :], sil[FR:P, m % 2, :], of("gate", n)[FR:P, :],
                                                  ALU.mult)
                        i.then_inc(S["fft"], 1)
                        wait("ffhi", m + 1)
                        if f < FB:
                            i = dve.tensor_tensor(fflo[:, f, :], fft[:, m % 2, :], ffhi[:, f, :].bitcast(F32),
                                                  ALU.subtract)
                        else:
                            i = dve.tensor_tensor(ffhi[FR:P, FB, :], fft[0:FR, m % 2, :],
                                                  ffhi[0:FR, FB, :].bitcast(F32), ALU.subtract)
                        i.then_inc(S["fflo"], 1)
                    elif kind == "down":
                        wait("down", n + 1)
                        if n == 0:
                            dve.wait_ge(s_out, 16 * NC * b + 1)
                        dve.scalar_tensor_tensor(obuf[:, n, :], of("down", n)[:, 0:C], r_yes[:, n:n + 1],
                                                 hbuf[:, n, :], ALU.mult, ALU.add).then_inc(S["u"], 1)
            assert chain[0] == DVE_CHAIN, chain[0]


_INS = ["L0_attn_x", "L0_attn_Wq", "L0_attn_bq", "L0_attn_Wk", "L0_attn_bk", "L0_attn_Wv", "L0_attn_bv", "L0_attn_Wo",
        "L0_attn_bo", "L0_ffn_w_router", "L0_ffn_b_router", "L0_ffn_norm1_w", "L0_ffn_wv", "L0_ffn_bv", "L0_ffn_wo",
        "L0_ffn_norm2_w", "L0_ffn_w_gate", "L0_ffn_w_up", "L0_ffn_w_down", "L0_c", "L0_wmod"]


def rope_tables():
    inv = (1.0 / 10000.0 ** (np.arange(HALF, dtype=np.float32) * 2.0 / D)).astype(np.float32)
    angle = np.arange(T, dtype=np.float32)[:, None] * inv[None, :]

    def lay(a):
        return np.ascontiguousarray(a.astype(np.float32).reshape(NT, P, HALF).transpose(1, 0, 2))

    return lay(np.cos(angle)), lay(np.sin(angle))


def kernel(**inputs):
    import concourse.bacc as bacc
    from concourse.bass_utils import run_bass_kernel_spmd

    nc = bacc.Bacc("TRN2", target_bir_lowering=False, num_devices=1)
    arrays = {name: np.ascontiguousarray(inputs[name]) for name in _INS}
    arrays["L0_ffn_b_router"] = arrays["L0_ffn_b_router"].reshape(1)
    arrays["rope_cos"], arrays["rope_sin"] = rope_tables()
    args = [nc.dram_tensor(f"in_{n}", a.shape, mybir.dt.from_np(a.dtype), kind="ExternalInput").ap()
            for n, a in arrays.items()]
    out = nc.dram_tensor("out_x", (B, T, C), F32, kind="ExternalOutput").ap()
    adaln_layer(nc, *args, out)
    r = run_bass_kernel_spmd(nc, [{f"in_{n}": a for n, a in arrays.items()}], core_ids=[0])
    return r.results[0]["out_x"]
```

```python
from contextlib import ExitStack

import concourse.bass as bass
import numpy as np
from concourse import mybir

F32 = mybir.dt.float32
F32R = mybir.dt.float32r
BF16 = mybir.dt.bfloat16
ALU = mybir.AluOpType
ACT = mybir.ActivationFunctionType
AX = mybir.AxisListType

P = 128
B, T, C = 4, 1024, 256
N_Q, H = 16, 4
G = N_Q // H
D = C // N_Q
HALF = D // 2
FF = 704
KB = C // P
NT = T // P
CH = 512
NC = T // CH
TPC = CH // P
QKV = 3 * H * D
FB = FF // P
FR = FF - FB * P
GUB = 2 * FB + 1
W1N = C + 2
QS = 3 * D
QP = 2 * QS
KR = QP + 2 * H
KSTEP = KR + QS
NEG = -1.0e30
LN_EPS, RMS_EPS = 1e-5, 1e-6

MAX_UNITS = []
for qt in range(NT):
    for k0 in range(0, (qt + 1) * P, CH):
        kn = min(CH, (qt + 1) * P - k0)
        hn = min(H, CH // kn)
        MAX_UNITS += [(qt, k0, kn, h0, hn) for h0 in range(0, H, hn)]
MAX_OF_CHUNK = [[u for u in MAX_UNITS if u[0] // TPC == c] for c in range(NC)]
P_UNITS = [(c, j, max(0, j - c * TPC) * P) for c in range(NC) for j in range((c + 1) * TPC)]

COST = dict(prob=1.5, pv=0.7, max=0.7, gateup=2.6, down=2.1, a=1.3, wo=0.5, hT=0.4, h2T=0.4, xT=0.4, qkv=0.8,
            stackT=1.1, norm1=3.0, weights=1.0, rope=1.0)


def merge(*streams):
    at = []
    for m, (stream, start, end) in enumerate(streams):
        total, spent = sum(COST.get(kind, 0.2) for kind, _ in stream), 0.0
        for kind, n in stream:
            cost = COST.get(kind, 0.2)
            at.append((start + (end - start) * (spent + cost / 2) / total, m, len(at), (kind, n)))
            spent += cost
    return [a[3] for a in sorted(at)]


def staggered(first, tiles, kinds_lags):
    last = max(lag for _, lag in kinds_lags)
    return [(kind, first + s - lag) for s in range(tiles + last) for kind, lag in kinds_lags if 0 <= s - lag < tiles]


def project_steps():
    out = [("weights", 0), ("norm1", 0)]
    lags = (("xT", 0), ("xlo", 0), ("qkv", 1), ("qkvb", 1))
    first, rest = staggered(0, TPC, lags), staggered(TPC, NT - TPC, lags)
    stacks = [[s for t in range(c * TPC, (c + 1) * TPC) for s in (("stackT", t), ("qT", t))] for c in range(NC)]
    out += first + [("rope", 0)] + merge((stacks[0], 0.2, 1.0), (rest, 0.0, 1.0)) + [("rope", 1)]
    maxima = [("max", (0, n)) for n in range(len(MAX_OF_CHUNK[0]))] + [("maxrow", 0)]
    return out + merge((stacks[1], 0.3, 1.0), (maxima, 0.0, 1.0))


def prob_steps(c):
    units = [n for n, u in enumerate(P_UNITS) if u[0] == c]
    out = staggered(units[0], len(units), (("prob", 0), ("pv", 1)))
    return out + [("ycopy", c), ("yT", c), ("ynT", c)]


def second_norm_steps(c):
    return staggered(c * TPC, TPC, (("wo", 0), ("x1", 0), ("norm2", 1), ("hT", 2), ("hlo", 2), ("a", 3),
                                    ("route", 3), ("h2", 4), ("h2T", 5), ("h2lo", 5)))


def ffn_steps(c):
    out = staggered(0, FB + 1, (("gateup", 0), ("fft", 1), ("split", 2)))
    out = [(kind, (c, f)) for kind, f in out]
    return out + staggered(c * TPC, TPC, (("down", 0), ("sum", 1)))


MAX_REST = [("max", (c, n)) for c in range(1, NC) for n in range(len(MAX_OF_CHUNK[c]))] + [("maxrow", 1)]
ATTEND = (merge((prob_steps(0) + second_norm_steps(0), 0.0, 1.0), (MAX_REST + prob_steps(1), 0.0, 1.0))
          + merge((second_norm_steps(1), 0.0, 1.0), (ffn_steps(0), 0.0, 1.0)))
PROJ = set(project_steps())
SEG = {"first": [(0, "A", *s) for s in project_steps()],
       "rows": [(0, "B", *s) for s in ATTEND] + [(1, "A", *s) if s in PROJ else (0, "B", *s) for s in merge(
           (project_steps(), 0.0, 1.0), (ffn_steps(1), 0.0, 1.0))],
       "last": [(0, "B", *s) for s in ATTEND + ffn_steps(1)]}
DVE_CHAIN = {"A": 1 + 1 + NC + 1, "B": NT + (NC - 1) * 2 + NC}
POOL_CHAIN = {"A": 1, "B": NT * 3 + NT * 2}
V_CSL, V_MOD, V_FWVT = 2, 8, 9


def adaln_layer(nc, x, Wq, bq, Wk, bk, Wv, bv, Wo, bo, w_router, b_router, n1, f_wv, f_bv, f_wo, n2,
                w_gate, w_up, w_down, c_in, wmod, rope_cos, rope_sin, out):
    ctx = ExitStack()
    with ctx:
        ctx.enter_context(nc.allow_non_contiguous_dma(reason="short vectors laid over partitions"))

        def sb(name, shape, dt=F32):
            return ctx.enter_context(nc.sbuf_tensor(name, shape, dt))

        def sem(name):
            return ctx.enter_context(nc.semaphore(name))

        mod_dram = nc.dram_tensor("mod_scratch", [B, 6 * C], F32, kind="Internal").ap()

        ident = sb("ident", [P, P])
        ident_b = sb("ident_b", [P, P], BF16)
        mask_qk = sb("mask_qk", [P, P], BF16)
        mask_kq = sb("mask_kq", [P, P], BF16)
        cos_t = sb("cos_t", [P, NT, HALF])
        sin_t = sb("sin_t", [P, NT, HALF])
        expo = sb("expo", [P, NT])
        eps_ln = sb("eps_ln", [P, NT])
        eps_rms = sb("eps_rms", [P, NT])
        Wqkv = sb("Wqkv", [P, KB, QKV])
        bqkv = sb("bqkv", [P, QKV])
        Wo_raw = sb("Wo_raw", [H * D + 1, C])
        W1hi = sb("W1hi", [P, KB, W1N], F32R)
        W1lo = sb("W1lo", [P, KB, W1N], F32R)
        b1 = sb("b1", [P, C])
        brout = sb("brout", [P, 1])
        guhi = sb("guhi", [P, KB, GUB, P], F32R)
        gulo = sb("gulo", [P, KB, GUB, P], F32R)
        wdhi = sb("wdhi", [P, FB + 1, C], F32R)
        wdlo = sb("wdlo", [P, FB + 1, C], F32R)
        n1col = sb("n1col", [P, KB])
        n2col = sb("n2col", [P, KB])
        bvcol = sb("bvcol", [P, KB])
        modA = sb("modA", [P, C])
        modB = sb("modB", [P, 3, C])
        modc = sb("modc", [P, 2, KB])
        Wqhi = sb("Wqhi", [P, KB, QKV], F32R)
        Wqlo = sb("Wqlo", [P, KB, QKV], F32R)
        bias_q = sb("bias_q", [P, QKV])
        Wo_b = sb("Wo_b", [H * D + 1, C])
        tok = sb("tok", [P, 6, NT * C])
        xbuf, xn, hbuf, hh, x1, obuf = (tok[:, n, :].rearrange("p (t c) -> p t c", t=NT) for n in range(6))
        h2 = xn
        fTh = sb("fTh", [P, TPC, KB, P], F32R)
        fTl = sb("fTl", [P, TPC, KB, P], F32R)
        scr = tok[:, 3, :].rearrange("p (m n) -> p m n", m=4)
        qk = scr[:, 0, :].rearrange("p (t h e i) -> p t h e i", t=TPC, h=2 * H, e=2)
        rt = scr[:, 1:3, :].rearrange("p a (b t h i) -> p (a b) t h i", b=2, t=TPC, h=2 * H)
        rot = scr[:, 3, :].rearrange("p (t h d) -> p t h d", t=TPC, h=2 * H)
        silfft = sb("silfft", [P, 4, CH])
        sil, fft = silfft[:, 0:2, :], silfft[:, 2:4, :]
        Qst = sb("Qst", [P, TPC, H, QS])
        Kst = sb("Kst", [P, TPC, H * KSTEP])
        QT = sb("QT", [KR, 2, T], F32R)
        KT = sb("KT", [KR, H, T], F32R)
        V = sb("V", [P, NT, H, 2 * D])
        mx = sb("mx", [P, NT, H])
        mxp = sb("mxp", [P, NT, H, 2])
        mt = sb("mt", [P, NT, H, 2])
        yT = sb("yT", [P, CH])
        rc = sb("rc", [P, TPC, H])
        ytm = sb("ytm", [P, TPC, H * D + 1])
        yT65 = sb("yT65", [H * D + 1, NT, P])
        st = sb("st", [P, NT, 6])
        tick = sb("tick", [P, 1])
        mv1 = sb("mv1", [P, NT, 2])
        mv2 = sb("mv2", [P, NT, 2])
        rstd1 = sb("rstd1", [P, NT])
        rstd2 = sb("rstd2", [P, NT])
        ms = sb("ms", [P, 2, NT])
        rs = sb("rs", [P, 2, NT])
        r_yes = sb("r_yes", [P, NT])
        r_no = sb("r_no", [P, NT])
        sq = sb("sq", [P, 2, C])

        def placed(name, shape, dt=F32):
            return stretch.enter_context(nc.sbuf_tensor(name, shape, dt))

        with ExitStack() as stretch:
            wg_st = placed("wg_st", [P, KB, FF])
            wu_st = placed("wu_st", [P, KB, FF])
            w1_st = placed("w1_st", [P, KB, W1N])
            fwvT = placed("fwvT", [P, KB, C])
        gTh = sb("gTh", [P, KB, T], F32R)
        gTl = sb("gTl", [P, KB, T], F32R)
        with ExitStack() as stretch:
            wm_st = placed("wm_st", [P, KB, 6 * C])
            wq_st = placed("wq_st", [P, KB, C])
            wk_st = placed("wk_st", [P, KB, H * D])
            wv_st = placed("wv_st", [P, KB, H * D])
            bb_st = placed("bb_st", [P, C + 2 * H * D])
            fwv_st = placed("fwv_st", [P, KB, C])
            fwo_st = placed("fwo_st", [P, KB, C])
        with ExitStack() as stretch:
            PT = placed("PT", [P, 2, H, CH])
        ffhi = sb("ffhi", [P, FB + 1, CH], F32R)
        fflo = sb("fflo", [P, FB, CH], F32R)

        bank = [ctx.enter_context(nc.psum_tensor(f"bank{n}", [P, CH], F32)) for n in range(8)]

        cT, cth, csl = (tok[:, 4, n * 8:n * 8 + 8].rearrange("p (k b) -> p k b", k=KB) for n in range(3))
        wd_st = tok[:, 5, 0:(FB + 1) * C].rearrange("p (k n) -> p k n", k=FB + 1)
        gabs = tok[0:B, 5, (FB + 1) * C:(FB + 3) * C].rearrange("b (m n) -> b m n", m=2)
        modr = silfft[0:B, 0:3, :].rearrange("b a n -> b (a n)")
        gsgn = silfft[0:B, 3, :].rearrange("b (m n) -> b m n", m=2)

        l_small, l_qkv, l_mod, l_ffn, l_gu, l_wd = (sem(n) for n in (
            "l_small", "l_qkv", "l_mod", "l_ffn", "l_gu", "l_wd"))
        s_const = sem("s_const")
        s_setA, s_setV, s_setP = sem("s_setA"), sem("s_setV"), sem("s_setP")
        s_modw = sem("s_modw")
        s_x, s_modA, s_modB = sem("s_x"), sem("s_modA"), sem("s_modB")
        s_out = sem("s_out")
        N = dict(
            bias_pe=1, biasq=1, wq=1,
            mv1=1, rstd1=1, xn=NT, xT=NT, xhi=NT, xlo=NT,
            qkv=NT, qkvb=NT, rope=NC, sthi=NC, stlo=NC,
            kTp=NT, qTp=NT, kT=NT, qT=NT,
            sc=len(MAX_UNITS), mxd=len(MAX_UNITS), mt=NC, mtp=NC, mrow=NC,
            st=H * len(P_UNITS), p=H * len(P_UNITS), pv=len(P_UNITS),
            yTs=NC, yTp=NC, ytm=NC, ynTp=NC, yn=NC,
            wo=NT, x1=NT, mv2=NT, rstd2=NT, xh=NT, h=NT, hb=NT, ms1=NT, rs1=NT,
            hTp=NT, hhi=NT, hlo=NT, a=NT, r=NT, hh=NT, ms2=NT, rs2=NT, hnr=NT,
            h2=NT, hsel=NT, h2Tp=NT, h2hi=NT, h2lo=NT,
            gu=NC * (FB + 1), up=NC * FB, sil=NC * (FB + 1), fft=NC * (FB + 1), ffhi=NC * (FB + 1),
            fflo=NC * (FB + 1), down=NT, u=NT, o=NT,
            dchainA=DVE_CHAIN["A"], dchainB=DVE_CHAIN["B"], pchainA=POOL_CHAIN["A"], pchainB=POOL_CHAIN["B"])
        S = {n: sem("s_" + n) for n in N}
        START = {"u": 1, "o": 1}

        BANK, before, last_in = {}, {}, [None] * 8

        def plan(seg):
            turn = [0, 0]

            def claim(r, kind, n, signal, count, half, banks=4):
                where = 4 * half + turn[half] % banks if banks else 3
                turn[half] += bool(banks)
                assert BANK.setdefault((kind, n), where) == where
                before[seg, kind, n] = last_in[where]
                last_in[where] = (signal, count, r)

            if seg != "first":
                last_in[0:4] = [None] * 4
            for r, group, kind, n in SEG[seg]:
                if kind == "weights":
                    turn[1] = 0
                    claim(r, "bias", 0, "biasq", 1, 1)
                elif kind == "xT":
                    claim(r, "xT", n, "xlo", n + 1, 1)
                elif kind == "qkv":
                    claim(r, "qkv", n, "qkvb", n + 1, 1)
                elif kind == "stackT":
                    claim(r, "kTp", n, "kT", n + 1, 1)
                    claim(r, "qTp", n, "qT", n + 1, 1)
                elif kind == "max":
                    claim(r, "max", n, "mxd", max_index(*n) + 1, 1)
                elif kind == "maxrow":
                    claim(r, "mtp", n, "mrow", n + 1, 1)
                elif kind == "prob":
                    for h in range(H):
                        claim(r, "st", (n, h), "p", n * H + h + 1, 0, 3)
                elif kind == "pv" and P_UNITS[n][1] == 0:
                    claim(r, "pv", P_UNITS[n][0], "yTs", P_UNITS[n][0] + 1, 0, 0)
                elif kind == "yT":
                    claim(r, "yTp", n, "ytm", n + 1, 1)
                elif kind == "ynT":
                    claim(r, "ynTp", n, "yn", n + 1, 1)
                elif kind == "wo":
                    claim(r, "wo", n, "x1", n + 1, 1)
                elif kind == "hT":
                    claim(r, "hTp", n, "hlo", n + 1, 1)
                elif kind == "a":
                    claim(r, "a", n, "hh", n + 1, 1)
                elif kind == "h2T":
                    claim(r, "h2Tp", n, "h2lo", n + 1, 1)
                elif kind == "gateup":
                    m = n[0] * (FB + 1) + n[1] + 1
                    if n == (0, 0):
                        turn[0] = 0
                    claim(r, "gate", n, "sil" if n[1] < FB else "fft", m, 0)
                    if n[1] < FB:
                        claim(r, "upp", n, "fft", m, 0)
                elif kind == "down":
                    claim(r, "down", n, "u", n + 1, 0)
            return last_in[4:]

        def max_index(c, n):
            return sum(len(m) for m in MAX_OF_CHUNK[:c]) + n

        first = plan("first")
        assert plan("rows") == [(signal, count, 1) for signal, count, _ in first]
        last_in[4:] = first
        plan("last")

        kst = Kst[:].rearrange("p t (h n) -> p t h n", h=H)

        def kst_head(h):
            return h * KSTEP - (h % 2) * QS

        def of(kind, n):
            return bank[BANK[kind, n]]

        def flat(ap):
            return ap.rearrange("p k n -> p (k n)")

        def by_block(ap):
            return ap.rearrange("p (k n) -> p k n", k=KB)

        block = ctx.enter_context(nc.Block())

        @block.sync
        def _(sp):
            def load_x(b):
                sp.dma_start(xbuf, x[bass.ds(b, 1), :, :].rearrange("o (t p) c -> p (o t) c", p=P)).then_inc(s_x, 16)

            load_x(0)
            for k in range(KB):
                sp.dma_start(cT[:, k, :], c_in[:, k * P:(k + 1) * P].rearrange("b p -> p b")).then_inc(l_mod, 16)
            sp.dma_start(wm_st[:], wmod.rearrange("(k p) n -> p k n", p=P)).then_inc(l_mod, 16)
            sp.dma_start(wq_st[:], Wq.rearrange("(k p) n -> p k n", p=P)).then_inc(l_qkv, 16)
            sp.dma_start(wk_st[:], Wk.rearrange("(k p) n -> p k n", p=P)).then_inc(l_qkv, 16)
            sp.dma_start(wv_st[:], Wv.rearrange("(k p) n -> p k n", p=P)).then_inc(l_qkv, 16)
            sp.dma_start(bb_st[:, 0:C], bq.partition_broadcast(P)).then_inc(l_qkv, 16)
            sp.dma_start(bb_st[:, C:C + 64], bk.partition_broadcast(P)).then_inc(l_qkv, 16)
            sp.dma_start(bb_st[:, C + 64:C + 128], bv.partition_broadcast(P)).then_inc(l_qkv, 16)
            sp.dma_start(cos_t[:], rope_cos).then_inc(l_small, 16)
            sp.dma_start(sin_t[:], rope_sin).then_inc(l_small, 16)
            sp.dma_start(Wo_raw[0:H * D, :], Wo).then_inc(l_small, 16)
            sp.dma_start(Wo_raw[H * D:H * D + 1, :], bo.unsqueeze(0)).then_inc(l_small, 16)
            sp.dma_start(brout[:], b_router.partition_broadcast(P)).then_inc(l_small, 16)
            sp.dma_start(fwv_st[:], f_wv.rearrange("(k p) n -> p k n", p=P)).then_inc(l_ffn, 16)
            sp.dma_start(fwo_st[:], f_wo.rearrange("(k p) n -> p k n", p=P)).then_inc(l_ffn, 16)
            sp.dma_start(n1col[:], n1.rearrange("(k p) -> p k", p=P)).then_inc(l_ffn, 16)
            sp.dma_start(n2col[:], n2.rearrange("(k p) -> p k", p=P)).then_inc(l_ffn, 16)
            sp.dma_start(bvcol[:], f_bv.rearrange("(k p) -> p k", p=P)).then_inc(l_ffn, 16)
            sp.dma_start(w1_st[:, :, C], w_router.rearrange("(k p) -> p k", p=P)).then_inc(l_ffn, 16)
            sp.dma_start(wd_st[:, 0:FB, :], w_down[0:FB * P, :].rearrange("(k p) n -> p k n", p=P)).then_inc(l_wd, 16)
            sp.dma_start(wd_st[0:FR, FB, :], w_down[FB * P:FF, :]).then_inc(l_wd, 16)
            sp.dma_start(wd_st[FR:P, FB, :], w_down[FB * P:FF, :]).then_inc(l_wd, 16)
            sp.dma_start(wg_st[:], w_gate.rearrange("(k p) n -> p k n", p=P)).then_inc(l_gu, 16)
            sp.dma_start(wu_st[:], w_up.rearrange("(k p) n -> p k n", p=P)).then_inc(l_gu, 16)
            sp.wait_ge(s_setV, V_MOD)
            sp.dma_start(mod_dram, modr).then_inc(s_modw, 16)
            sp.wait_ge(s_modw, 16)
            sp.sem_inc(s_out, 1)
            sp.sem_inc(S["o"], 1)

            def load_modA(b):
                for v in range(2):
                    sp.dma_start(modc[:, v, :], mod_dram[bass.ds(b, 1), v * C:(v + 1) * C].rearrange(
                        "o (k p) -> p (o k)", p=P)).then_inc(s_modA, 16)
                sp.dma_start(modA[:], mod_dram[bass.ds(b, 1), 2 * C:3 * C].rearrange("o n -> (o n)"
                             ).partition_broadcast(P)).then_inc(s_modA, 16)

            def load_modB(b):
                sp.dma_start(modB[:].rearrange("p v n -> p (v n)"), mod_dram[bass.ds(b, 1), 3 * C:6 * C].rearrange(
                    "o n -> (o n)").partition_broadcast(P)).then_inc(s_modB, 16)

            def store(b):
                for c in range(NC):
                    sp.wait_ge(S["o"], b * N["o"] + (c + 1) * TPC + START["o"])
                    sp.dma_start(out[bass.ds(b, 1), c * CH:(c + 1) * CH, :].rearrange("o (t p) c -> p (o t) c", p=P),
                                 obuf[:, c * TPC:(c + 1) * TPC, :]).then_inc(s_out, 16)

            load_modA(0)
            load_modB(0)
            with sp.Fori(0, B - 1) as b:
                sp.wait_ge(S["biasq"], b * N["biasq"] + 1)
                load_modA(b + 1)
                sp.wait_ge(S["x1"], b * N["x1"] + NT)
                load_x(b + 1)
                store(b)
                load_modB(b + 1)
            store(B - 1)
            sp.wait_ge(s_out, 16 * NC * B + 1)

        @block.gpsimd
        def _(pool):
            pool.memset(ident[:], 0.0)
            pool.memset(mask_qk[:], 0.0)
            pool.memset(mask_kq[:], 0.0)
            pool.memset(expo[:], -0.5)
            pool.memset(eps_ln[:], LN_EPS)
            pool.memset(eps_rms[:], RMS_EPS)
            pool.memset(V[:], 0.0)
            pool.memset(Kst[:], 0.0)
            pool.memset(ytm[:], 1.0).then_inc(s_const, 1)
            pool.wait_ge(s_const, 1)
            pool.affine_select(out=ident[:], in_=ident[:], compare_op=ALU.not_equal, fill=1.0, base=0,
                               pattern=[[-1, P]], channel_multiplier=1)
            pool.affine_select(out=mask_qk[:], in_=mask_qk[:], compare_op=ALU.is_ge, fill=NEG, base=0,
                               pattern=[[-1, P]], channel_multiplier=1)
            pool.affine_select(out=mask_kq[:], in_=mask_kq[:], compare_op=ALU.is_ge, fill=NEG, base=0,
                               pattern=[[1, P]], channel_multiplier=-1)
            for h in range(H):
                at = kst_head(h) + QP + 2 * h
                pool.memset(Kst[:, :, at:at + 2], 1.0)
            pool.memset(V[:, :, :, D:D + 1], 1.0).then_inc(s_const, 1)
            pool.wait_ge(s_const, 2)
            pool.tensor_copy(ident_b[:], ident[:]).then_inc(s_const, 1)

            def part(seg, b):
                r = 0
                group = "A"
                chain = {g: 0 for g in {step[1] for step in SEG[seg]}}
                def wait(name, k):
                    pool.wait_ge(S[name], (b + r) * N[name] + k + START.get(name, 0))

                def then(i):
                    i.then_inc(S["pchain" + group], 1)
                    chain[group] += 1
                    wait("pchain" + group, chain[group])

                def rsqrt(dst, src, eps, done):
                    then(pool.tensor_tensor(dst, src, eps, ALU.add))
                    pool.tensor_tensor(dst, dst, expo[:, 0:dst.shape[1]], ALU.pow).then_inc(done, 1)

                for r, group, kind, n in SEG[seg]:
                    if kind == "norm1":
                        wait("mv1", 1)
                        rsqrt(rstd1[:], mv1[:, :, 1], eps_ln[:], S["rstd1"])
                    elif kind == "x1":
                        wait("mv2", n + 1)
                        rsqrt(rstd2[:, n:n + 1], mv2[:, n, 1:2], eps_ln[:, 0:1], S["rstd2"])
                    elif kind == "norm2":
                        if n == 0:
                            pool.wait_ge(s_modB, 16 * b + 16)
                        wait("xh", n + 1)
                        then(pool.tensor_tensor(hbuf[:, n, :], hbuf[:, n, :], modB[:, 1, :], ALU.mult))
                        pool.tensor_tensor(hbuf[:, n, :], hbuf[:, n, :], modB[:, 0, :], ALU.add).then_inc(S["h"], 1)
                        wait("h", n + 1)
                        pool.tensor_tensor(hh[:, n, :], hbuf[:, n, :], b1[:], ALU.add).then_inc(S["hb"], 1)
                        wait("ms1", n + 1)
                        rsqrt(rs[:, 0, n:n + 1], ms[:, 0, n:n + 1], eps_rms[:, 0:1], S["rs1"])
                    elif kind == "route":
                        wait("ms2", n + 1)
                        rsqrt(rs[:, 1, n:n + 1], ms[:, 1, n:n + 1], eps_rms[:, 0:1], S["rs2"])
                    elif kind == "sum":
                        wait("u", n + 1)
                        then(pool.tensor_tensor(obuf[:, n, :], obuf[:, n, :], modB[:, 2, :], ALU.mult))
                        pool.tensor_tensor(obuf[:, n, :], obuf[:, n, :], x1[:, n, :], ALU.add).then_inc(S["o"], 1)
                assert all(chain[g] == POOL_CHAIN[g] for g in chain), chain

            part("first", 0)
            with pool.Fori(0, B - 1) as b:
                part("rows", b)
            part("last", B - 1)

        @block.tensor
        def _(pe):
            pe.wait_ge(s_setV, V_CSL)
            for n in range(3):
                for k in range(KB):
                    i = pe.matmul(bank[n][0:B, :], csl[:, k, :], wm_st[:, k, n * CH:(n + 1) * CH],
                                  start=(k == 0), stop=(k == KB - 1))
            i.then_inc(s_setP, 1)
            def three_pass(o, hi, lo, whi, wlo, first, last):
                pe.matmul(o, hi, whi, start=first, stop=False)
                pe.matmul(o, hi, wlo, start=False, stop=False)
                return pe.matmul(o, lo, whi, start=False, stop=last)

            def part(seg, b):
                r = 0
                def wait(name, k):
                    pe.wait_ge(S[name], (b + r) * N[name] + k + START.get(name, 0))

                def take(kind, n, **needs):
                    if before[seg, kind, n] is not None:
                        signal, k, ahead = before[seg, kind, n]
                        if signal not in needs:
                            pe.wait_ge(S[signal], (b + ahead) * N[signal] + k + START.get(signal, 0))
                        elif ahead == r:
                            needs[signal] = max(needs[signal], k)
                    for name, k in needs.items():
                        wait(name, k)
                    return of(kind, n)

                if seg != "first":
                    wait("u", 0)
                for r, group, kind, n in SEG[seg]:
                    if kind == "weights":
                        pe.wait_ge(s_modA, (b + r) * 48 + 48)
                        o = take("bias", 0)
                        for k in range(KB):
                            i = pe.matmul(o[:, 0:QKV], modc[:, 0, k:k + 1].to_broadcast([P, P]), Wqkv[:, k, :],
                                          start=(k == 0), stop=(k == KB - 1))
                        i.then_inc(S["bias_pe"], 1)
                    elif kind == "xT":
                        wait("xn", n + 1)
                        o = take("xT", n)
                        for k in range(KB):
                            i = pe.transpose(o[:, k * P:(k + 1) * P], xn[:, n, k * P:(k + 1) * P], ident[:])
                        i.then_inc(S["xT"], 1)
                    elif kind == "qkv":
                        if n == 0:
                            wait("wq", 1)
                        o = take("qkv", n, xlo=n + 1)
                        for k in range(KB):
                            i = three_pass(o[:, 0:QKV], fTh[:, n % TPC, k, :], fTl[:, n % TPC, k, :], Wqhi[:, k, :], Wqlo[:, k, :],
                                           k == 0, k == KB - 1)
                        i.then_inc(S["qkv"], 1)
                    elif kind == "stackT":
                        if n % TPC == 0:
                            wait("sthi", n // TPC + 1)
                            wait("stlo", n // TPC + 1)
                        o = take("kTp", n)
                        for h in range(H):
                            at = kst_head(h)
                            i = pe.transpose(o[0:KR, h * P:(h + 1) * P], Kst[:, n % TPC, at:at + KR], ident[:])
                        i.then_inc(S["kTp"], 1)
                        o = take("qTp", n)
                        for q in range(2):
                            i = pe.transpose(o[0:QP, q * P:(q + 1) * P], Qst[:, n % TPC, 2 * q:2 * q + 2, :].rearrange(
                                "p h d -> p (h d)"), ident[:])
                        i.then_inc(S["qTp"], 1)
                    elif kind == "max":
                        qt, k0, kn, h0, hn = MAX_OF_CHUNK[n[0]][n[1]]
                        o = take("max", n, kT=qt + 1, qT=qt + 1)
                        diag = k0 + kn == (qt + 1) * P
                        for h in range(h0, h0 + hn):
                            col = (h - h0) * kn
                            i = pe.matmul(o[:, col:col + kn], QT[0:QP, h // 2, qt * P:(qt + 1) * P],
                                          KT[0:QP, h, k0:k0 + kn], start=True, stop=not diag)
                            if diag:
                                i = pe.matmul(o[:, col + kn - P:col + kn], ident_b[:], mask_qk[:],
                                              start=False, stop=True)
                        i.then_inc(S["sc"], 1)
                    elif kind == "maxrow":
                        wait("mt", n + 1)
                        o = take("mtp", n)
                        for t in range(TPC):
                            i = pe.transpose(o[0:2 * H, t * P:(t + 1) * P],
                                             mt[:, n * TPC + t, :, :].rearrange("p h e -> p (h e)"), ident[:])
                        i.then_inc(S["mtp"], 1)
                    elif kind == "prob":
                        c, j, q0 = P_UNITS[n]
                        if j == 0:
                            wait("mrow", c + 1)
                        for h in range(H):
                            o = take("st", (n, h))
                            diag = j >= c * TPC
                            i = pe.matmul(o[:, 0:CH - q0], KT[:, h, j * P:(j + 1) * P],
                                          QT[:, h // 2, c * CH + q0:(c + 1) * CH], start=True, stop=not diag)
                            if diag:
                                i = pe.matmul(o[:, 0:P], ident_b[:], mask_kq[:], start=False, stop=True)
                            i.then_inc(S["st"], 1)
                    elif kind == "pv":
                        c, j, q0 = P_UNITS[n]
                        wait("p", H * (n + 1))
                        o = take("pv", c) if j == 0 else of("pv", c)
                        for h in range(H):
                            i = pe.matmul(o[h * 2 * D:(h + 1) * 2 * D, q0:CH], V[:, j, h, :],
                                          PT[:, n % 2, h, 0:CH - q0], start=(j == 0), stop=(q0 == CH - P),
                                          skip_group_check=True)
                        i.then_inc(S["pv"], 1)
                    elif kind == "yT":
                        wait("yTs", n + 1)
                        o = take("yTp", n)
                        for t in range(TPC):
                            i = pe.transpose(o[:, t * P:(t + 1) * P], yT[:, t * P:(t + 1) * P], ident[:])
                        i.then_inc(S["yTp"], 1)
                    elif kind == "ynT":
                        o = take("ynTp", n, ytm=n + 1)
                        for t in range(TPC):
                            i = pe.transpose(o[0:H * D + 1, t * P:(t + 1) * P], ytm[:, t, :], ident[:])
                        i.then_inc(S["ynTp"], 1)
                    elif kind == "wo":
                        o = take("wo", n, yn=n // TPC + 1)
                        pe.matmul(o[:, 0:C], yT65[:, n, :], Wo_b[:], start=True, stop=True).then_inc(S["wo"], 1)
                    elif kind == "hT":
                        wait("h", n + 1)
                        o = take("hTp", n)
                        for k in range(KB):
                            i = pe.transpose(o[:, k * P:(k + 1) * P], hbuf[:, n, k * P:(k + 1) * P], ident[:])
                        i.then_inc(S["hTp"], 1)
                    elif kind == "a":
                        o = take("a", n, hlo=n + 1)
                        for k in range(KB):
                            i = three_pass(o[:, 0:W1N], fTh[:, n % TPC, k, :], fTl[:, n % TPC, k, :], W1hi[:, k, :], W1lo[:, k, :],
                                           k == 0, k == KB - 1)
                        i.then_inc(S["a"], 1)
                    elif kind == "h2T":
                        wait("h2", n + 1)
                        o = take("h2Tp", n)
                        for k in range(KB):
                            i = pe.transpose(o[:, k * P:(k + 1) * P], h2[:, n, k * P:(k + 1) * P], ident[:])
                        i.then_inc(S["h2Tp"], 1)
                    elif kind == "gateup":
                        c, f = n
                        if f == 0:
                            wait("h2lo", (c + 1) * TPC)
                        cols = slice(c * CH, (c + 1) * CH)
                        for what, blk in ((("gate", f), ("upp", FB + f)) if f < FB else (("gate", 2 * FB),)):
                            o = take(what, n)
                            for k in range(KB):
                                pe.matmul(o[:], guhi[:, k, blk, :], gTh[:, k, cols], start=(k == 0), stop=False)
                                pe.matmul(o[:], guhi[:, k, blk, :], gTl[:, k, cols], start=False, stop=False)
                                i = pe.matmul(o[:], gulo[:, k, blk, :], gTh[:, k, cols], start=False,
                                              stop=(k == KB - 1))
                            i.then_inc(S["gu" if what == "gate" else "up"], 1)
                    elif kind == "down":
                        c, t = n // TPC, n % TPC
                        if t == 0:
                            wait("fflo", (c + 1) * (FB + 1))
                        o = take("down", n)[:, 0:C]
                        cols = slice(t * P, (t + 1) * P)
                        for f in range(FB):
                            three_pass(o, ffhi[:, f, cols], fflo[:, f, cols], wdhi[:, f, :], wdlo[:, f, :],
                                       f == 0, False)
                        pe.matmul(o, ffhi[:, FB, cols], wdhi[:, FB, :], start=False, stop=False)
                        pe.matmul(o, ffhi[:, FB, cols], wdlo[:, FB, :], start=False, stop=True
                                  ).then_inc(S["down"], 1)

            part("first", 0)
            pe.wait_ge(l_ffn, 96)
            pe.wait_ge(s_const, 3)
            for d in range(KB):
                for k in range(KB):
                    i = pe.transpose(bank[3][:, (d * KB + k) * P:(d * KB + k + 1) * P],
                                     fwv_st[:, k, d * P:(d + 1) * P], ident[:])
            i.then_inc(s_setP, 1)
            pe.wait_ge(s_setV, V_FWVT)
            for k in range(KB):
                for d in range(KB):
                    pe.matmul(bank[k][:, 0:C], fwvT[:, d, k * P:(k + 1) * P], fwo_st[:, d, :],
                              start=(d == 0), stop=(d == KB - 1))
            for d in range(KB):
                i = pe.matmul(bank[2][:, 0:C], bvcol[:, d:d + 1].to_broadcast([P, P]), fwo_st[:, d, :],
                              start=(d == 0), stop=(d == KB - 1))
            i.then_inc(s_setP, 1)
            with pe.Fori(0, B - 1) as b:
                part("rows", b)
            part("last", B - 1)

        @block.scalar
        def _(act):
            act.wait_ge(l_mod, 48)
            act.activation(cth, cT, ACT.Tanh, scale=0.5).then_inc(s_setA, 1)
            def part(seg, b):
                r = 0
                def wait(name, k):
                    act.wait_ge(S[name], (b + r) * N[name] + k + START.get(name, 0))

                for r, group, kind, n in SEG[seg]:
                    if kind == "xT":
                        wait("xT", n + 1)
                        if n >= TPC:
                            wait("qkv", n - TPC + 1)
                        act.activation(flat(fTh[:, n % TPC, :, :]), of("xT", n)[:, 0:C], ACT.Copy).then_inc(S["xhi"], 1)
                    elif kind == "rope":
                        wait("rope", n + 1)
                        if n > 0:
                            wait("qTp", n * TPC)
                        for at in (0, D):
                            act.activation(Qst[:, :, :, at:at + D].bitcast(F32R), rot[:, :, 0:H, :], ACT.Copy)
                        for at in (0, 2 * D):
                            i = act.activation(kst[:, :, :, at:at + D].bitcast(F32R), rot[:, :, H:2 * H, :], ACT.Copy)
                        i.then_inc(S["sthi"], 1)
                    elif kind == "stackT":
                        wait("kTp", n + 1)
                        act.activation(KT[:, :, n * P:(n + 1) * P],
                                       of("kTp", n)[0:KR, :].rearrange("p (h n) -> p h n", h=H), ACT.Copy
                                       ).then_inc(S["kT"], 1)
                    elif kind == "maxrow":
                        wait("mtp", n + 1)
                        for q in range(2):
                            i = act.activation(QT[QP:KR, q, n * CH:(n + 1) * CH], of("mtp", n)[0:2 * H, :], ACT.Copy)
                        i.then_inc(S["mrow"], 1)
                    elif kind == "prob":
                        c, j, q0 = P_UNITS[n]
                        if n >= 2:
                            wait("pv", n - 1)
                        for h in range(H):
                            wait("st", n * H + h + 1)
                            act.activation(PT[:, n % 2, h, 0:CH - q0], of("st", (n, h))[:, 0:CH - q0], ACT.Exp,
                                           scale=float(D) ** -0.5).then_inc(S["p"], 1)
                    elif kind == "ycopy":
                        wait("pv", [m + 1 for m, u in enumerate(P_UNITS) if u[0] == n][-1])
                        if n > 0:
                            wait("yTp", n)
                        act.activation(yT[:], of("pv", n)[:], ACT.Copy).then_inc(S["yTs"], 1)
                    elif kind == "ynT":
                        wait("ynTp", n + 1)
                        act.activation(yT65[:, n * TPC:(n + 1) * TPC, :].rearrange("p t n -> p (t n)"),
                                       of("ynTp", n)[0:H * D + 1, :], ACT.Copy).then_inc(S["yn"], 1)
                    elif kind == "norm2":
                        wait("h", n + 1)
                        if n > 0:
                            wait("ms1", n)
                        act.activation(sq[:, 0, :], hbuf[:, n, :], ACT.Square, scale=float(C) ** -0.5,
                                       accum_out=ms[:, 0, n:n + 1]).then_inc(S["ms1"], 1)
                    elif kind == "hT":
                        wait("hTp", n + 1)
                        if n >= TPC:
                            wait("a", n - TPC + 1)
                        act.activation(flat(fTh[:, n % TPC, :, :]), of("hTp", n)[:, 0:C], ACT.Copy).then_inc(S["hhi"], 1)
                    elif kind == "route":
                        wait("hh", n + 1)
                        if n > 0:
                            wait("ms2", n)
                        act.activation(sq[:, 1, :], hh[:, n, :], ACT.Square, scale=float(C) ** -0.5,
                                       accum_out=ms[:, 1, n:n + 1]).then_inc(S["ms2"], 1)
                        act.activation(hbuf[:, n, :], hbuf[:, n, :], ACT.Copy, scale=r_no[:, n:n + 1]
                                       ).then_inc(S["hnr"], 1)
                    elif kind == "h2T":
                        wait("h2Tp", n + 1)
                        act.activation(gTh[:, :, n * P:(n + 1) * P], by_block(of("h2Tp", n)[:, 0:C]), ACT.Copy
                                       ).then_inc(S["h2hi"], 1)
                    elif kind == "gateup":
                        c, f = n
                        m = c * (FB + 1) + f
                        wait("gu", m + 1)
                        if m >= 2:
                            wait("fft", m - 1)
                        if f < FB:
                            act.activation(sil[:, m % 2, :], of("gate", n)[:], ACT.Silu).then_inc(S["sil"], 1)
                        else:
                            act.activation(sil[FR:P, m % 2, :], of("gate", n)[0:FR, :], ACT.Silu
                                           ).then_inc(S["sil"], 1)
                    elif kind == "split":
                        c, f = n
                        m = c * (FB + 1) + f
                        wait("fft", m + 1)
                        if f == 0 and c > 0:
                            wait("down", c * TPC)
                        rows = P if f < FB else FR
                        act.activation(ffhi[0:rows, f, :], fft[0:rows, m % 2, :], ACT.Copy).then_inc(S["ffhi"], 1)

            part("first", 0)
            with act.Fori(0, B - 1) as b:
                part("rows", b)
            part("last", B - 1)

        @block.vector
        def _(dve):
            done = [0]

            def setup(i):
                i.then_inc(s_setV, 1)
                done[0] += 1
                return done[0]

            def setup_then(i):
                k = setup(i)
                dve.wait_ge(s_setV, k)

            dve.wait_ge(s_setA, 1)
            setup_then(dve.scalar_tensor_tensor(csl, cth, 1.0, cT, ALU.add, ALU.mult))
            assert setup(dve.tensor_scalar(csl, csl, 0.5, None, ALU.mult)) == V_CSL
            dve.wait_ge(l_qkv, 96)
            groups = [(wq_st[:, k, :], wk_st[:, k, :], wv_st[:, k, :], Wqkv[:, k, :]) for k in range(KB)]
            groups += [(bb_st[:, 0:C], bb_st[:, C:C + H * D], bb_st[:, C + H * D:C + 2 * H * D], bqkv[:])]
            for wq, wk, wv, w in groups:
                for e in range(2):
                    dve.tensor_reduce(w[:, 0:H * D].rearrange("p (h e i) -> p e h i", h=H, e=2)[:, e],
                                      wq.rearrange("p (h g i e) -> p e h i g", h=H, g=G, e=2)[:, e], AX.X, ALU.add)
                    dve.tensor_copy(w[:, H * D:2 * H * D].rearrange("p (h e i) -> p e h i", h=H, e=2)[:, e],
                                    wk.rearrange("p (h i e) -> p e h i", h=H, e=2)[:, e])
                i = dve.tensor_copy(w[:, 2 * H * D:QKV], wv)
            setup(i)
            dve.wait_ge(s_setP, 1)
            for n in range(3):
                i = dve.tensor_copy(modr[:, n * CH:(n + 1) * CH], bank[n][0:B, :])
            setup_then(i)
            rows = modr.rearrange("b (m v n) -> b m v n", m=2, v=3)
            dve.tensor_scalar(rows[:, :, 1, :], rows[:, :, 1, :], 1.0, None, ALU.add)
            setup_then(dve.tensor_scalar(gsgn, rows[:, :, 2, :], 0.0, 2.0, ALU.is_ge, ALU.mult))
            setup_then(dve.scalar_tensor_tensor(gabs, gsgn, -1.0, rows[:, :, 2, :], ALU.add, ALU.mult))
            setup_then(dve.tensor_scalar(gabs, gabs, 0.25, None, ALU.max))
            assert setup(dve.scalar_tensor_tensor(rows[:, :, 2, :], gsgn, -1.0, gabs, ALU.add, ALU.mult)
                         ) == V_MOD
            dve.wait_ge(l_small, 80)
            dve.wait_ge(s_const, 3)

            def part(seg, b):
                r = 0
                group = "A"
                chain = {g: 0 for g in {step[1] for step in SEG[seg]}}

                def wait(name, k):
                    dve.wait_ge(S[name], (b + r) * N[name] + k + START.get(name, 0))

                def then(i):
                    i.then_inc(S["dchain" + group], 1)
                    chain[group] += 1
                    wait("dchain" + group, chain[group])


                for r, group, kind, n in SEG[seg]:
                    if kind == "weights":
                        dve.wait_ge(s_modA, (b + r) * 48 + 48)
                        for k in range(KB):
                            i = dve.tensor_scalar(Wqhi[:, k, :], Wqkv[:, k, :], modc[:, 1, k:k + 1], None, ALU.mult)
                        then(i)
                        for k in range(KB):
                            i = dve.scalar_tensor_tensor(Wqlo[:, k, :], Wqkv[:, k, :], modc[:, 1, k:k + 1],
                                                         Wqhi[:, k, :].bitcast(F32), ALU.mult, ALU.subtract)
                        i.then_inc(S["wq"], 1)
                        dve.tensor_tensor(Wo_b[:], Wo_raw[:], modA[0:H * D + 1, :], ALU.mult)
                        wait("bias_pe", 1)
                        dve.tensor_tensor(bias_q[:], of("bias", 0)[:, 0:QKV], bqkv[:], ALU.add
                                          ).then_inc(S["biasq"], 1)
                    elif kind == "norm1":
                        dve.wait_ge(s_x, (b + r) * 16 + 16)
                        for t in range(NT):
                            i = dve.bn_stats(st[:, t, :], xbuf[:, t, :])
                        then(i)
                        dve.memset(tick[:], 0.0)
                        for t in range(NT):
                            i = dve.bn_aggr(mv1[:, t, :], st[:, t, :])
                        i.then_inc(S["mv1"], 1)
                        wait("rstd1", 1)
                        for t in range(NT):
                            dve.tensor_scalar(xn[:, t, :], xbuf[:, t, :], mv1[:, t, 0:1], rstd1[:, t:t + 1],
                                              ALU.subtract, ALU.mult).then_inc(S["xn"], 1)
                    elif kind == "xlo":
                        wait("xhi", n + 1)
                        dve.tensor_tensor(flat(fTl[:, n % TPC, :, :]), of("xT", n)[:, 0:C],
                                          flat(fTh[:, n % TPC, :, :]).bitcast(F32), ALU.subtract).then_inc(S["xlo"], 1)
                    elif kind == "qkvb":
                        wait("qkv", n + 1)
                        o = of("qkv", n)
                        dve.tensor_tensor(qk[:, n % TPC, :, :, :].rearrange("p h e i -> p (h e i)"),
                                          o[:, 0:2 * H * D], bias_q[:, 0:2 * H * D], ALU.add)
                        dve.tensor_tensor(V[:, n, :, 0:D], o[:, 2 * H * D:QKV].rearrange("p (h d) -> p h d", h=H),
                                          bias_q[:, 2 * H * D:QKV].rearrange("p (h d) -> p h d", h=H), ALU.add
                                          ).then_inc(S["qkvb"], 1)
                    elif kind == "rope":
                        wait("qkvb", (n + 1) * TPC)
                        if n > 0:
                            wait("sthi", n)
                            wait("qTp", n * TPC)
                        ts = slice(n * TPC, (n + 1) * TPC)
                        cs = cos_t[:, ts, :].unsqueeze(2).to_broadcast([P, TPC, 2 * H, HALF])
                        sn = sin_t[:, ts, :].unsqueeze(2).to_broadcast([P, TPC, 2 * H, HALF])
                        ev, od = qk[:, :, :, 0, :], qk[:, :, :, 1, :]
                        for m, (u, v) in enumerate(((ev, cs), (od, sn), (ev, sn), (od, cs))):
                            i = dve.tensor_tensor(rt[:, m], u, v, ALU.mult)
                        then(i)
                        dve.tensor_tensor(rot[:, :, :, 0:HALF], rt[:, 0], rt[:, 1], ALU.subtract)
                        dve.tensor_tensor(rot[:, :, :, HALF:D], rt[:, 2], rt[:, 3], ALU.add).then_inc(S["rope"], 1)
                        wait("sthi", n + 1)
                        dve.tensor_tensor(Qst[:, :, :, 2 * D:3 * D].bitcast(F32R), rot[:, :, 0:H, :],
                                          Qst[:, :, :, 0:D], ALU.subtract)
                        dve.tensor_tensor(kst[:, :, :, D:2 * D].bitcast(F32R), rot[:, :, H:2 * H, :],
                                          kst[:, :, :, 0:D], ALU.subtract).then_inc(S["stlo"], 1)
                    elif kind == "qT":
                        wait("qTp", n + 1)
                        dve.tensor_copy(QT[0:QP, :, n * P:(n + 1) * P],
                                        by_block(of("qTp", n)[0:QP, 0:2 * P])).then_inc(S["qT"], 1)
                    elif kind == "max":
                        qt, k0, kn, h0, hn = MAX_OF_CHUNK[n[0]][n[1]]
                        wait("sc", max_index(*n) + 1)
                        dst = mx[:, qt, h0:h0 + hn] if qt < TPC else mxp[:, qt, h0:h0 + hn, k0 // CH]
                        dve.tensor_reduce(dst, of("max", n)[:, 0:hn * kn].rearrange("p (h k) -> p h k", h=hn), AX.X,
                                          ALU.max).then_inc(S["mxd"], 1)
                    elif kind == "maxrow":
                        ts = slice(n * TPC, (n + 1) * TPC)
                        wait("mxd", max_index(n, len(MAX_OF_CHUNK[n])))
                        if n > 0:
                            then(dve.tensor_reduce(mx[:, ts, :], mxp[:, ts, :, :], AX.X, ALU.max))
                        then(dve.tensor_scalar(mt[:, ts, :, 0].bitcast(F32R), mx[:, ts, :], -1.0, None, ALU.mult))
                        dve.scalar_tensor_tensor(mt[:, ts, :, 1].bitcast(F32R), mx[:, ts, :], -1.0,
                                                 mt[:, ts, :, 0], ALU.mult, ALU.subtract).then_inc(S["mt"], 1)
                    elif kind == "yT":
                        wait("yTp", n + 1)
                        if n > 0:
                            wait("ynTp", n)
                        o = of("yTp", n)[:].rearrange("p (t h d) -> p t h d", t=TPC, h=H)
                        then(dve.reciprocal(rc[:], o[:, :, :, D]))
                        dve.tensor_tensor(ytm[:, :, 0:H * D].rearrange("p t (h d) -> p t h d", h=H), o[:, :, :, 0:D],
                                          rc[:].unsqueeze(3).to_broadcast([P, TPC, H, D]), ALU.mult
                                          ).then_inc(S["ytm"], 1)
                    elif kind == "x1":
                        if n == 0:
                            wait("o", 0)
                        wait("wo", n + 1)
                        dve.tensor_tensor(x1[:, n, :], of("wo", n)[:, 0:C], xbuf[:, n, :], ALU.add
                                          ).then_inc(S["x1"], 1)
                        wait("x1", n + 1)
                        then(dve.bn_stats(st[:, n, :], x1[:, n, :]))
                        dve.memset(tick[:], 0.0)
                        dve.bn_aggr(mv2[:, n, :], st[:, n, :]).then_inc(S["mv2"], 1)
                    elif kind == "norm2":
                        wait("rstd2", n + 1)
                        dve.tensor_scalar(hbuf[:, n, :], x1[:, n, :], mv2[:, n, 0:1], rstd2[:, n:n + 1],
                                          ALU.subtract, ALU.mult).then_inc(S["xh"], 1)
                    elif kind == "hlo":
                        wait("hhi", n + 1)
                        dve.tensor_tensor(flat(fTl[:, n % TPC, :, :]), of("hTp", n)[:, 0:C],
                                          flat(fTh[:, n % TPC, :, :]).bitcast(F32), ALU.subtract).then_inc(S["hlo"], 1)
                    elif kind == "route":
                        wait("a", n + 1)
                        wait("rs1", n + 1)
                        wait("hb", n + 1)
                        o = of("a", n)
                        dve.tensor_scalar(r_no[:, n:n + 1], o[:, C:C + 1], brout[:], 0.0, ALU.add, ALU.is_le)
                        dve.tensor_scalar(r_yes[:, n:n + 1], o[:, C:C + 1], brout[:], 0.0, ALU.add, ALU.is_gt)
                        dve.scalar_tensor_tensor(hh[:, n, :], o[:, 0:C], rs[:, 0, n:n + 1], hh[:, n, :],
                                                 ALU.mult, ALU.add).then_inc(S["hh"], 1)
                    elif kind == "h2":
                        wait("rs2", n + 1)
                        dve.tensor_scalar(h2[:, n, :], hh[:, n, :], rs[:, 1, n:n + 1], None, ALU.mult
                                          ).then_inc(S["h2"], 1)
                        wait("hnr", n + 1)
                        dve.scalar_tensor_tensor(hbuf[:, n, :], hh[:, n, :], r_yes[:, n:n + 1], hbuf[:, n, :],
                                                 ALU.mult, ALU.add).then_inc(S["hsel"], 1)
                    elif kind == "h2lo":
                        wait("h2hi", n + 1)
                        cols = slice(n * P, (n + 1) * P)
                        dve.tensor_tensor(gTl[:, :, cols], by_block(of("h2Tp", n)[:, 0:C]),
                                          gTh[:, :, cols].bitcast(F32), ALU.subtract).then_inc(S["h2lo"], 1)
                    elif kind == "fft":
                        c, f = n
                        m = c * (FB + 1) + f
                        wait("sil", m + 1)
                        if m >= 2:
                            wait("fflo", m - 1)
                        if f < FB:
                            wait("up", c * FB + f + 1)
                            i = dve.tensor_tensor(fft[:, m % 2, :], sil[:, m % 2, :], of("upp", n)[:], ALU.mult)
                        else:
                            i = dve.tensor_tensor(fft[0:FR, m % 2, :], sil[FR:P, m % 2, :], of("gate", n)[FR:P, :],
                                                  ALU.mult)
                        i.then_inc(S["fft"], 1)
                    elif kind == "split":
                        c, f = n
                        m = c * (FB + 1) + f
                        wait("ffhi", m + 1)
                        if f < FB:
                            i = dve.tensor_tensor(fflo[:, f, :], fft[:, m % 2, :], ffhi[:, f, :].bitcast(F32),
                                                  ALU.subtract)
                        else:
                            i = dve.tensor_tensor(ffhi[FR:P, FB, :], fft[0:FR, m % 2, :],
                                                  ffhi[0:FR, FB, :].bitcast(F32), ALU.subtract)
                        i.then_inc(S["fflo"], 1)
                    elif kind == "sum":
                        wait("down", n + 1)
                        if n == 0:
                            dve.wait_ge(s_out, 16 * NC * b + 1)
                        dve.scalar_tensor_tensor(obuf[:, n, :], of("down", n)[:, 0:C], r_yes[:, n:n + 1],
                                                 hbuf[:, n, :], ALU.mult, ALU.add).then_inc(S["u"], 1)
                assert all(chain[g] == DVE_CHAIN[g] for g in chain), chain

            part("first", 0)
            dve.wait_ge(s_setP, 2)
            assert setup(dve.tensor_copy(flat(fwvT[:]), bank[3][:])) == V_FWVT
            dve.wait_ge(s_setP, 3)
            for k in range(KB):
                dve.tensor_scalar(w1_st[:, k, 0:C], bank[k][:, 0:C], n1col[:, k:k + 1], None, ALU.mult)
                dve.memset(w1_st[:, k, C + 1:C + 2], 0.0)
            setup_then(dve.tensor_copy(b1[:], bank[2][:, 0:C]))
            setup_then(dve.tensor_copy(W1hi[:], w1_st[:]))
            dve.tensor_tensor(W1lo[:], w1_st[:], W1hi[:].bitcast(F32), ALU.subtract)
            dve.wait_ge(l_gu, 32)
            pieces = []
            for k in range(KB):
                for j, w in enumerate((wg_st, wu_st)):
                    pieces.append((w[:, k, 0:FB * P], k, slice(j * FB, (j + 1) * FB), slice(0, P)))
                    pieces.append((w[:, k, FB * P:FF], k, slice(2 * FB, GUB), slice(j * FR, (j + 1) * FR)))
            for src, k, blk, cols in pieces:
                hi = guhi[:, k, blk, cols]
                i = dve.tensor_scalar(hi, src.rearrange("p (f n) -> p f n", n=hi.shape[2]), n2col[:, k:k + 1], None,
                                      ALU.mult)
            setup_then(i)
            for src, k, blk, cols in pieces:
                hi = guhi[:, k, blk, cols]
                dve.scalar_tensor_tensor(gulo[:, k, blk, cols], src.rearrange("p (f n) -> p f n", n=hi.shape[2]),
                                         n2col[:, k:k + 1], hi.bitcast(F32), ALU.mult, ALU.subtract)
            dve.wait_ge(l_wd, 48)
            setup_then(dve.tensor_copy(wdhi[:], wd_st))
            setup_then(dve.tensor_tensor(wdlo[:], wd_st, wdhi[:].bitcast(F32), ALU.subtract))
            dve.tensor_copy(tick[:], brout[:]).then_inc(S["u"], 1)
            with dve.Fori(0, B - 1) as b:
                part("rows", b)
            part("last", B - 1)



_INS = ["L0_attn_x", "L0_attn_Wq", "L0_attn_bq", "L0_attn_Wk", "L0_attn_bk", "L0_attn_Wv", "L0_attn_bv", "L0_attn_Wo",
        "L0_attn_bo", "L0_ffn_w_router", "L0_ffn_b_router", "L0_ffn_norm1_w", "L0_ffn_wv", "L0_ffn_bv", "L0_ffn_wo",
        "L0_ffn_norm2_w", "L0_ffn_w_gate", "L0_ffn_w_up", "L0_ffn_w_down", "L0_c", "L0_wmod"]


def rope_tables():
    inv = (1.0 / 10000.0 ** (np.arange(HALF, dtype=np.float32) * 2.0 / D)).astype(np.float32)
    angle = np.arange(T, dtype=np.float32)[:, None] * inv[None, :]

    def lay(a):
        return np.ascontiguousarray(a.astype(np.float32).reshape(NT, P, HALF).transpose(1, 0, 2))

    return lay(np.cos(angle)), lay(np.sin(angle))


def kernel(**inputs):
    import concourse.bacc as bacc
    from concourse.bass_utils import run_bass_kernel_spmd

    nc = bacc.Bacc("TRN2", target_bir_lowering=False, num_devices=1)
    arrays = {name: np.ascontiguousarray(inputs[name]) for name in _INS}
    arrays["L0_ffn_b_router"] = arrays["L0_ffn_b_router"].reshape(1)
    arrays["rope_cos"], arrays["rope_sin"] = rope_tables()
    args = [nc.dram_tensor(f"in_{n}", a.shape, mybir.dt.from_np(a.dtype), kind="ExternalInput").ap()
            for n, a in arrays.items()]
    out = nc.dram_tensor("out_x", (B, T, C), F32, kind="ExternalOutput").ap()
    adaln_layer(nc, *args, out)
    r = run_bass_kernel_spmd(nc, [{f"in_{n}": a for n, a in arrays.items()}], core_ids=[0])
    return r.results[0]["out_x"]
```

```python
from contextlib import ExitStack

import concourse.bass as bass
import numpy as np
from concourse import mybir

F32 = mybir.dt.float32
F32R = mybir.dt.float32r
BF16 = mybir.dt.bfloat16
ALU = mybir.AluOpType
ACT = mybir.ActivationFunctionType
AX = mybir.AxisListType

P = 128
B, T, C = 4, 1024, 256
N_Q, H = 16, 4
G = N_Q // H
D = C // N_Q
HALF = D // 2
FF = 704
KB = C // P
NT = T // P
CH = 512
NC = T // CH
TPC = CH // P
QKV = 3 * H * D
FB = FF // P
FR = FF - FB * P
GUB = 2 * FB + 1
W1N = C + 2
QS = 3 * D
QP = 2 * QS
KR = QP + 2 * H
KSTEP = KR + QS
NEG = -1.0e30
LN_EPS, RMS_EPS = 1e-5, 1e-6

MAX_UNITS = []
for qt in range(NT):
    for k0 in range(0, (qt + 1) * P, CH):
        kn = min(CH, (qt + 1) * P - k0)
        hn = min(H, CH // kn)
        MAX_UNITS += [(qt, k0, kn, h0, hn) for h0 in range(0, H, hn)]
MAX_OF_CHUNK = [[u for u in MAX_UNITS if u[0] // TPC == c] for c in range(NC)]
P_UNITS = [(c, j, max(0, j - c * TPC) * P) for c in range(NC) for j in range((c + 1) * TPC)]

TILES, BLOCKS = list(range(NT)), [(c, f) for c in range(NC) for f in range(FB + 1)]
UNITS = [[n for n, u in enumerate(P_UNITS) if u[0] == c] for c in range(NC)]
GROUPS = {
    "A": dict(stats=[0, 1], norm1=TILES, weights=[0], xT=TILES, xlo=TILES, qkv=TILES, qkvb=TILES, rope=[0, 1],
              split1=[0, 1], stackT=TILES, qT=TILES, max=[(c, n) for c in range(NC)
                                                          for n in range(len(MAX_OF_CHUNK[c]))], maxrow=[0, 1],
              prob=UNITS[0], pv=UNITS[0], ycopy=[0], yT=[0], ynT=[0]),
    "B": dict(prob=UNITS[1], pv=UNITS[1], ycopy=[1], yT=[1], ynT=[1], wo=TILES, x1=TILES, norm2=TILES, hT=TILES,
              hlo=TILES, rs1=TILES, a=TILES, route=TILES, h2=TILES, h2T=TILES, h2lo=TILES, gate=BLOCKS,
              up=[(c, f) for c, f in BLOCKS if f < FB], fft=BLOCKS, split=BLOCKS, down=TILES, sum=TILES),
    "S": dict(setw=[0], mod=[0], prep=list(range(8)))}
FIRST = """
stats setw norm1 mod norm1 norm1 prep xT norm1 xlo xT xlo xT stats prep weights xT prep xlo xlo qkv qkv norm1
qkv qkv norm1 qkvb xT qkvb norm1 qkvb xT xT prep qkvb norm1 rope xlo xT xlo xlo xlo qkv qkv qkvb split1 qkvb qkv
qkv qkvb stackT stackT qkvb stackT qT stackT qT qT qT rope max max max max split1 max prep max max max prep
stackT qT max max max stackT stackT maxrow qT qT max max max max max max prob prep max max max max max max max
stackT qT max max pv max max max prob max prob max prep pv prob max pv max pv max max max max max ycopy yT ynT
maxrow
""".split()
ROW = """
wo wo x1 prob wo wo prob pv prob pv prob x1 pv norm2 hT prob x1 norm2 norm2 hT pv x1 hlo rs1 a prob hT pv prob
norm2 stats hT hlo rs1 hlo pv route a prob rs1 hlo route h2 rs1 a pv pv ycopy route h2 a route yT h2T h2T ynT h2
h2lo h2T h2lo h2 wo h2T wo h2lo x1 h2lo wo wo x1 norm2 x1 x1 weights gate gate hT norm1 up up norm2 hT hlo fft
norm2 stats gate rs1 hlo fft norm1 norm1 up split a rs1 split hT gate norm2 norm1 hlo route up a fft xT fft
route xlo hT h2 h2 split gate rs1 split hlo up rs1 xT h2T xlo gate fft h2lo a fft split split a qkv down h2T
route route h2lo sum down h2 xT h2T norm1 down h2 qkvb h2lo xlo h2T qkv norm1 h2lo qkvb xT sum xlo qkv norm1
gate norm1 qkvb xT sum qkv down xT gate sum xT xlo qkvb xlo up xT rope qkv qkvb up qkv xlo xlo qkv split1 qkv
qkvb qkvb stackT stackT qkvb stackT fft qT qT stackT fft qT gate qT rope split max gate max max max up split1
max fft max up split max max max gate max stackT qT fft max stackT stackT qT stackT maxrow qT qT max gate max
max max max up split max max max split prob max fft prob fft pv max prob max pv max max split split prob pv max
max pv max max down sum max ycopy max max max down sum max max max max down sum max max yT down ynT maxrow sum
""".split()
LAST = """
wo prob wo wo prob pv x1 prob norm2 x1 pv prob hT x1 norm2 pv wo prob hT norm2 x1 pv hlo rs1 hlo a prob hT pv
prob rs1 norm2 hlo rs1 a route hT pv route a prob hlo pv pv route h2 rs1 h2 a ycopy h2 h2T route h2lo yT h2 h2T
h2T ynT h2lo h2lo h2T wo wo h2lo wo x1 x1 gate up gate norm2 hT up norm2 fft x1 split hlo wo gate rs1 a norm2 hT
x1 up fft route hlo split hT fft gate up norm2 fft rs1 h2 hlo split split gate gate hT rs1 hlo rs1 up a fft fft
split split a route route a route down h2T down h2 h2 sum h2lo down h2 h2T h2lo h2T h2lo h2T sum down h2lo gate
sum up sum gate up fft fft gate split split up gate fft up fft split gate split gate up fft fft split split down
down down sum sum down sum sum
""".split()


def segment(kinds, *groups):
    left = {}
    for ahead, name in groups:
        for kind, every in GROUPS[name].items():
            left.setdefault(kind, []).extend((ahead, name, kind, n) for n in every)
    steps = [left[kind].pop(0) for kind in kinds]
    assert not any(left.values())
    return steps


SEG = {"first": segment(FIRST, (0, "S"), (0, "A")), "rows": segment(ROW, (0, "B"), (1, "A")),
       "last": segment(LAST, (0, "B"))}
DVE_CHAIN = {"S": 0, "A": 1 + NC + NC + 1 + (NC - 1) * 2 + 1, "B": NT + NC - 1}
POOL_CHAIN = {"S": 0, "A": NC, "B": NT * 3 + NT * 2}
V_CSL, V_SETW, V_MOD, V_FWVT = 2, 3, 8, 9


def adaln_layer(nc, x, Wq, bq, Wk, bk, Wv, bv, Wo, bo, w_router, b_router, n1, f_wv, f_bv, f_wo, n2,
                w_gate, w_up, w_down, c_in, wmod, rope_cos, rope_sin, out):
    ctx = ExitStack()
    with ctx:
        ctx.enter_context(nc.allow_non_contiguous_dma(reason="short vectors laid over partitions"))

        def sb(name, shape, dt=F32):
            return ctx.enter_context(nc.sbuf_tensor(name, shape, dt))

        def sem(name):
            return ctx.enter_context(nc.semaphore(name))

        mod_dram = nc.dram_tensor("mod_scratch", [B, 6 * C], F32, kind="Internal").ap()

        ident = sb("ident", [P, P])
        ident_b = sb("ident_b", [P, P], BF16)
        mask_qk = sb("mask_qk", [P, P], BF16)
        mask_kq = sb("mask_kq", [P, P], BF16)
        cos_t = sb("cos_t", [P, NT, HALF])
        sin_t = sb("sin_t", [P, NT, HALF])
        expo = sb("expo", [P, NT])
        eps_ln = sb("eps_ln", [P, NT])
        eps_rms = sb("eps_rms", [P, NT])
        Wqkv = sb("Wqkv", [P, KB, QKV])
        bqkv = sb("bqkv", [P, QKV])
        Wo_raw = sb("Wo_raw", [H * D + 1, C])
        W1hi = sb("W1hi", [P, KB, W1N], F32R)
        W1lo = sb("W1lo", [P, KB, W1N], F32R)
        b1 = sb("b1", [P, C])
        brout = sb("brout", [P, 1])
        guhi = sb("guhi", [P, KB, GUB, P], F32R)
        gulo = sb("gulo", [P, KB, GUB, P], F32R)
        wdhi = sb("wdhi", [P, FB + 1, C], F32R)
        wdlo = sb("wdlo", [P, FB + 1, C], F32R)
        n1col = sb("n1col", [P, KB])
        n2col = sb("n2col", [P, KB])
        bvcol = sb("bvcol", [P, KB])
        modA = sb("modA", [P, C])
        modB = sb("modB", [P, 3, C])
        modc = sb("modc", [P, 2, KB])
        Wqhi = sb("Wqhi", [P, KB, QKV], F32R)
        Wqlo = sb("Wqlo", [P, KB, QKV], F32R)
        bias_q = sb("bias_q", [P, QKV])
        Wo_b = sb("Wo_b", [H * D + 1, C])
        tok = sb("tok", [P, 6, NT * C])
        xbuf, xn, hbuf, hh, x1, obuf = (tok[:, n, :].rearrange("p (t c) -> p t c", t=NT) for n in range(6))
        h2 = xn
        PT0 = tok[:, 1:4:2, :].rearrange("p s (h n) -> p s h n", h=H)
        fTh = sb("fTh", [P, TPC, KB, P], F32R)
        fTl = sb("fTl", [P, TPC, KB, P], F32R)
        scr = tok[:, 3, :].rearrange("p (m n) -> p m n", m=4)
        qk = scr[:, 0, :].rearrange("p (t h e i) -> p t h e i", t=TPC, h=2 * H, e=2)
        rt = scr[:, 1:3, :].rearrange("p a (b t h i) -> p (a b) t h i", b=2, t=TPC, h=2 * H)
        rot = scr[:, 3, :].rearrange("p (t h d) -> p t h d", t=TPC, h=2 * H)
        silfft = sb("silfft", [P, 4, CH])
        sil, fft = silfft[:, 0:2, :], silfft[:, 2:4, :]
        Qst = sb("Qst", [P, TPC, H, QS])
        Kst = sb("Kst", [P, TPC, H * KSTEP])
        QT = sb("QT", [KR, 2, T], F32R)
        KT = sb("KT", [KR, H, T], F32R)
        V = sb("V", [P, NT, H, 2 * D])
        mx = sb("mx", [P, NT, H])
        mxp = sb("mxp", [P, NT, H, 2])
        mt = sb("mt", [P, NT, H, 2])
        yT = sb("yT", [P, CH])
        rc = sb("rc", [P, TPC, H])
        ytm = sb("ytm", [P, TPC, H * D + 1])
        yT65 = sb("yT65", [H * D + 1, NT, P])
        st1 = sb("st1", [P, NT, 6])
        st = sb("st", [P, NT, 6])
        tick = sb("tick", [P, 1])
        mv1 = sb("mv1", [P, NT, 2])
        mv2 = sb("mv2", [P, NT, 2])
        rstd1 = sb("rstd1", [P, NT])
        rstd2 = sb("rstd2", [P, NT])
        ms = sb("ms", [P, 2, NT])
        rs = sb("rs", [P, 2, NT])
        r_yes = sb("r_yes", [P, NT])
        r_no = sb("r_no", [P, NT])
        sq = sb("sq", [P, 2, C])

        def placed(name, shape, dt=F32):
            return stretch.enter_context(nc.sbuf_tensor(name, shape, dt))

        with ExitStack() as stretch:
            wg_st = placed("wg_st", [P, KB, FF])
            wu_st = placed("wu_st", [P, KB, FF])
            w1_st = placed("w1_st", [P, KB, W1N])
            fwvT = placed("fwvT", [P, KB, C])
        gTh = sb("gTh", [P, KB, T], F32R)
        gTl = sb("gTl", [P, KB, T], F32R)
        with ExitStack() as stretch:
            wm_st = placed("wm_st", [P, KB, 6 * C])
            wq_st = placed("wq_st", [P, KB, C])
            wk_st = placed("wk_st", [P, KB, H * D])
            wv_st = placed("wv_st", [P, KB, H * D])
            bb_st = placed("bb_st", [P, C + 2 * H * D])
            fwv_st = placed("fwv_st", [P, KB, C])
            fwo_st = placed("fwo_st", [P, KB, C])
        with ExitStack() as stretch:
            PT1 = placed("PT1", [P, 2, H, CH])
        PT = (PT0, PT1)
        ffhi = sb("ffhi", [P, FB + 1, CH], F32R)
        fflo = sb("fflo", [P, FB, CH], F32R)

        bank = [ctx.enter_context(nc.psum_tensor(f"bank{n}", [P, CH], F32)) for n in range(8)]

        cT, cth, csl = (tok[:, 4, n * 8:n * 8 + 8].rearrange("p (k b) -> p k b", k=KB) for n in range(3))
        wd_st = tok[:, 5, 0:(FB + 1) * C].rearrange("p (k n) -> p k n", k=FB + 1)
        gabs = tok[0:B, 5, (FB + 1) * C:(FB + 3) * C].rearrange("b (m n) -> b m n", m=2)
        modr = silfft[0:B, 0:3, :].rearrange("b a n -> b (a n)")
        gsgn = silfft[0:B, 3, :].rearrange("b (m n) -> b m n", m=2)

        l_small, l_qkv, l_mod, l_ffn, l_gu, l_wd = (sem(n) for n in (
            "l_small", "l_qkv", "l_mod", "l_ffn", "l_gu", "l_wd"))
        s_const = sem("s_const")
        s_setA, s_setV, s_setP = sem("s_setA"), sem("s_setV"), sem("s_setP")
        s_setG = sem("s_setG")
        s_modw = sem("s_modw")
        s_x, s_modA, s_modB = [sem(f"s_xin{c}") for c in range(NC)], sem("s_modA"), sem("s_modB")
        s_out = sem("s_out")
        N = dict(
            bias_pe=1, biasq=1, wq=1,
            mv1=NC, rstd1=NC, xn=NT, xT=NT, xhi=NT, xlo=NT,
            qkv=NT, qkvb=NT, rope=NC, sthi=NC, stlo=NC,
            kTp=NT, qTp=NT, kT=NT, qT=NT,
            sc=len(MAX_UNITS), mxd=len(MAX_UNITS), mt=NC, mtp=NC, mrow=NC,
            st=H * len(P_UNITS), p=H * len(P_UNITS), pv=len(P_UNITS),
            yTs=NC, yTp=NC, ytm=NC, ynTp=NC, yn=NC,
            wo=NT, x1=NT, mv2=NT, rstd2=NT, xh=NT, h=NT, hb=NT, ms1=NT, rs1=NT,
            hTp=NT, hhi=NT, hlo=NT, a=NT, r=NT, hh=NT, ms2=NT, rs2=NT, hnr=NT,
            h2=NT, hsel=NT, h2Tp=NT, h2hi=NT, h2lo=NT,
            gate=NC * (FB + 1), up=NC * FB, sil=NC * (FB + 1), fft=NC * (FB + 1), ffhi=NC * (FB + 1),
            fflo=NC * (FB + 1), down=NT, u=NT, o=NT,
            dchainA=DVE_CHAIN["A"], dchainB=DVE_CHAIN["B"], pchainA=POOL_CHAIN["A"], pchainB=POOL_CHAIN["B"])
        S = {n: sem("s_" + n) for n in N}
        START = {"u": 1, "o": 1}

        BANK, before = {}, {}

        LOW, ONE, HIGH = (0, 1, 2), (3,), (4, 5, 6, 7)

        def plan(seg, held):
            turn, held = {}, list(held)

            def claim(r, kind, n, signal, count, banks):
                turn[banks] = turn.get(banks, -1) + 1
                where = banks[turn[banks] % len(banks)]
                BANK[seg, kind, n] = where
                before[seg, kind, n] = held[where]
                held[where] = [(signal, count, r)]

            for r, group, kind, n in SEG[seg]:
                if kind == "weights":
                    claim(r, "bias", 0, "biasq", 1, HIGH)
                elif kind == "xT":
                    claim(r, "xT", n, "xlo", n + 1, HIGH)
                elif kind == "qkv":
                    claim(r, "qkv", n, "qkvb", n + 1, HIGH)
                elif kind == "stackT":
                    claim(r, "kTp", n, "kT", n + 1, HIGH)
                    claim(r, "qTp", n, "qT", n + 1, HIGH)
                elif kind == "max":
                    claim(r, "max", n, "mxd", max_index(*n) + 1, HIGH)
                elif kind == "maxrow":
                    claim(r, "mtp", n, "mrow", n + 1, HIGH)
                elif kind == "prob":
                    for h in range(H):
                        claim(r, "st", (n, h), "p", n * H + h + 1, LOW if P_UNITS[n][0] else HIGH)
                elif kind == "pv" and P_UNITS[n][1] == 0:
                    claim(r, "pv", P_UNITS[n][0], "yTs", P_UNITS[n][0] + 1, ONE)
                elif kind == "yT":
                    claim(r, "yTp", n, "ytm", n + 1, HIGH)
                elif kind == "ynT":
                    claim(r, "ynTp", n, "yn", n + 1, HIGH)
                elif kind == "wo":
                    claim(r, "wo", n, "x1", n + 1, HIGH)
                elif kind == "hT":
                    claim(r, "hTp", n, "hlo", n + 1, HIGH)
                elif kind == "a":
                    claim(r, "a", n, "hh", n + 1, HIGH)
                elif kind == "h2T":
                    claim(r, "h2Tp", n, "h2lo", n + 1, HIGH)
                elif kind == "gate":
                    claim(r, kind, n, "sil" if n[1] < FB else "fft", n[0] * (FB + 1) + n[1] + 1, LOW)
                elif kind == "up":
                    claim(r, kind, n, "fft", n[0] * (FB + 1) + n[1] + 1, LOW)
                elif kind == "down":
                    claim(r, "down", n, "u", n + 1, LOW)
            return held

        def max_index(c, n):
            return sum(len(m) for m in MAX_OF_CHUNK[:c]) + n

        after_first = plan("first", [[]] * 8)
        after_row = plan("rows", [[]] * 8)
        assert all(ahead == 1 for held in after_row[3:] for _, _, ahead in held)
        entry = [[]] * 3
        for held in zip(after_first[3:], after_row[3:]):
            counts = {}
            for signal, count, _ in held[0] + held[1]:
                counts[signal] = max(count, counts.get(signal, 0))
            entry.append([(signal, count, 0) for signal, count in counts.items()])
        plan("rows", entry)
        plan("last", entry)

        kst = Kst[:].rearrange("p t (h n) -> p t h n", h=H)

        def kst_head(h):
            return h * KSTEP - (h % 2) * QS

        def of(seg, kind, n):
            return bank[BANK[seg, kind, n]]

        def flat(ap):
            return ap.rearrange("p k n -> p (k n)")

        def by_block(ap):
            return ap.rearrange("p (k n) -> p k n", k=KB)

        pieces = [((w[:, k, 0:FB * P], k, slice(j * FB, (j + 1) * FB), slice(0, P)),
                   (w[:, k, FB * P:FF], k, slice(2 * FB, GUB), slice(j * FR, (j + 1) * FR)))
                  for k in range(KB) for j, w in enumerate((wg_st, wu_st))]

        staged = [w for k in range(KB) for w in (wg_st, wu_st)]

        block = ctx.enter_context(nc.Block())

        @block.sync
        def _(sp):
            def load_x(b, c):
                sp.dma_start(xbuf[:, c * TPC:(c + 1) * TPC, :], x[bass.ds(b, 1), c * CH:(c + 1) * CH, :].rearrange(
                    "o (t p) c -> p (o t) c", p=P)).then_inc(s_x[c], 16)

            for k in range(KB):
                sp.dma_start(cT[:, k, :], c_in[:, k * P:(k + 1) * P].rearrange("b p -> p b")).then_inc(l_mod, 16)
            load_x(0, 0)
            sp.dma_start(wm_st[:], wmod.rearrange("(k p) n -> p k n", p=P)).then_inc(l_mod, 16)
            sp.dma_start(wq_st[:], Wq.rearrange("(k p) n -> p k n", p=P)).then_inc(l_qkv, 16)
            sp.dma_start(wk_st[:], Wk.rearrange("(k p) n -> p k n", p=P)).then_inc(l_qkv, 16)
            sp.dma_start(wv_st[:], Wv.rearrange("(k p) n -> p k n", p=P)).then_inc(l_qkv, 16)
            sp.dma_start(bb_st[:, 0:C], bq.partition_broadcast(P)).then_inc(l_qkv, 16)
            sp.dma_start(bb_st[:, C:C + 64], bk.partition_broadcast(P)).then_inc(l_qkv, 16)
            sp.dma_start(bb_st[:, C + 64:C + 128], bv.partition_broadcast(P)).then_inc(l_qkv, 16)
            load_x(0, 1)
            sp.dma_start(cos_t[:], rope_cos).then_inc(l_small, 16)
            sp.dma_start(sin_t[:], rope_sin).then_inc(l_small, 16)
            sp.dma_start(Wo_raw[0:H * D, :], Wo).then_inc(l_small, 16)
            sp.dma_start(Wo_raw[H * D:H * D + 1, :], bo.unsqueeze(0)).then_inc(l_small, 16)
            sp.dma_start(brout[:], b_router.partition_broadcast(P)).then_inc(l_small, 16)
            sp.dma_start(fwv_st[:], f_wv.rearrange("(k p) n -> p k n", p=P)).then_inc(l_ffn, 16)
            sp.dma_start(fwo_st[:], f_wo.rearrange("(k p) n -> p k n", p=P)).then_inc(l_ffn, 16)
            sp.dma_start(n1col[:], n1.rearrange("(k p) -> p k", p=P)).then_inc(l_ffn, 16)
            sp.dma_start(n2col[:], n2.rearrange("(k p) -> p k", p=P)).then_inc(l_ffn, 16)
            sp.dma_start(bvcol[:], f_bv.rearrange("(k p) -> p k", p=P)).then_inc(l_ffn, 16)
            sp.dma_start(w1_st[:, :, C], w_router.rearrange("(k p) -> p k", p=P)).then_inc(l_ffn, 16)
            sp.dma_start(wd_st[:, 0:FB, :], w_down[0:FB * P, :].rearrange("(k p) n -> p k n", p=P)).then_inc(l_wd, 16)
            sp.dma_start(wd_st[0:FR, FB, :], w_down[FB * P:FF, :]).then_inc(l_wd, 16)
            sp.dma_start(wd_st[FR:P, FB, :], w_down[FB * P:FF, :]).then_inc(l_wd, 16)
            sp.dma_start(wg_st[:], w_gate.rearrange("(k p) n -> p k n", p=P)).then_inc(l_gu, 16)
            sp.dma_start(wu_st[:], w_up.rearrange("(k p) n -> p k n", p=P)).then_inc(l_gu, 16)
            sp.wait_ge(s_setV, V_MOD)
            sp.dma_start(mod_dram, modr).then_inc(s_modw, 16)
            sp.wait_ge(s_modw, 16)
            sp.sem_inc(s_out, 1)
            sp.sem_inc(S["o"], 1)

            def load_modA(b):
                for v in range(2):
                    sp.dma_start(modc[:, v, :], mod_dram[bass.ds(b, 1), v * C:(v + 1) * C].rearrange(
                        "o (k p) -> p (o k)", p=P)).then_inc(s_modA, 16)
                sp.dma_start(modA[:], mod_dram[bass.ds(b, 1), 2 * C:3 * C].rearrange("o n -> (o n)"
                             ).partition_broadcast(P)).then_inc(s_modA, 16)

            def load_modB(b):
                sp.dma_start(modB[:].rearrange("p v n -> p (v n)"), mod_dram[bass.ds(b, 1), 3 * C:6 * C].rearrange(
                    "o n -> (o n)").partition_broadcast(P)).then_inc(s_modB, 16)

            def store(b):
                for c in range(NC):
                    sp.wait_ge(S["o"], b * N["o"] + (c + 1) * TPC + START["o"])
                    sp.dma_start(out[bass.ds(b, 1), c * CH:(c + 1) * CH, :].rearrange("o (t p) c -> p (o t) c", p=P),
                                 obuf[:, c * TPC:(c + 1) * TPC, :]).then_inc(s_out, 16)

            load_modA(0)
            load_modB(0)
            with sp.Fori(0, B - 1) as b:
                sp.wait_ge(S["biasq"], b * N["biasq"] + 1)
                load_modA(b + 1)
                for c in range(NC):
                    sp.wait_ge(S["x1"], b * N["x1"] + (c + 1) * TPC)
                    load_x(b + 1, c)
                store(b)
                load_modB(b + 1)
            store(B - 1)
            sp.wait_ge(s_out, 16 * NC * B + 1)

        @block.gpsimd
        def _(pool):
            pool.memset(ident[:], 0.0)
            pool.memset(mask_qk[:], 0.0)
            pool.memset(mask_kq[:], 0.0)
            pool.memset(expo[:], -0.5)
            pool.memset(eps_ln[:], LN_EPS)
            pool.memset(eps_rms[:], RMS_EPS)
            pool.memset(V[:], 0.0)
            pool.memset(Kst[:], 0.0)
            pool.memset(ytm[:], 1.0).then_inc(s_const, 1)
            pool.wait_ge(s_const, 1)
            pool.affine_select(out=ident[:], in_=ident[:], compare_op=ALU.not_equal, fill=1.0, base=0,
                               pattern=[[-1, P]], channel_multiplier=1)
            pool.affine_select(out=mask_qk[:], in_=mask_qk[:], compare_op=ALU.is_ge, fill=NEG, base=0,
                               pattern=[[-1, P]], channel_multiplier=1)
            pool.affine_select(out=mask_kq[:], in_=mask_kq[:], compare_op=ALU.is_ge, fill=NEG, base=0,
                               pattern=[[1, P]], channel_multiplier=-1)
            for h in range(H):
                at = kst_head(h) + QP + 2 * h
                pool.memset(Kst[:, :, at:at + 2], 1.0)
            pool.memset(V[:, :, :, D:D + 1], 1.0).then_inc(s_const, 1)
            pool.wait_ge(s_const, 2)
            pool.tensor_copy(ident_b[:], ident[:]).then_inc(s_const, 1)

            def part(seg, b):
                r = 0
                group = "A"
                chain = {g: 0 for g in {step[1] for step in SEG[seg]}}
                def wait(name, k):
                    pool.wait_ge(S[name], (b + r) * N[name] + k + START.get(name, 0))

                def then(i):
                    i.then_inc(S["pchain" + group], 1)
                    chain[group] += 1
                    wait("pchain" + group, chain[group])

                def rsqrt(dst, src, eps, done):
                    then(pool.tensor_tensor(dst, src, eps, ALU.add))
                    pool.tensor_tensor(dst, dst, expo[:, 0:dst.shape[1]], ALU.pow).then_inc(done, 1)

                for r, group, kind, n in SEG[seg]:
                    if kind == "prep" and 2 <= n < 2 + len(pieces):
                        pool.wait_ge(s_setA, 2 * n - 1)
                        for src, k, blk, cols in pieces[n - 2]:
                            hi = guhi[:, k, blk, cols]
                            i = pool.tensor_tensor(gulo[:, k, blk, cols], src.rearrange(
                                "p (f n) -> p f n", n=hi.shape[2]), hi.bitcast(F32), ALU.subtract)
                        i.then_inc(s_setG, 1)
                    elif kind == "prep" and n == 2 + len(pieces):
                        pool.wait_ge(s_setA, 2 * n - 2)
                        pool.tensor_tensor(wdlo[:], wd_st, wdhi[:].bitcast(F32), ALU.subtract).then_inc(s_setG, 1)
                    elif kind == "stats":
                        wait("mv1", n + 1)
                        ts = slice(n * TPC, (n + 1) * TPC)
                        rsqrt(rstd1[:, ts], mv1[:, ts, 1], eps_ln[:, ts], S["rstd1"])
                    elif kind == "x1":
                        wait("mv2", n + 1)
                        rsqrt(rstd2[:, n:n + 1], mv2[:, n, 1:2], eps_ln[:, 0:1], S["rstd2"])
                    elif kind == "norm2":
                        if n == 0:
                            pool.wait_ge(s_modB, 16 * b + 16)
                        wait("xh", n + 1)
                        then(pool.tensor_tensor(hbuf[:, n, :], hbuf[:, n, :], modB[:, 1, :], ALU.mult))
                        pool.tensor_tensor(hbuf[:, n, :], hbuf[:, n, :], modB[:, 0, :], ALU.add).then_inc(S["h"], 1)
                        wait("h", n + 1)
                        pool.tensor_tensor(hh[:, n, :], hbuf[:, n, :], b1[:], ALU.add).then_inc(S["hb"], 1)
                    elif kind == "rs1":
                        wait("ms1", n + 1)
                        rsqrt(rs[:, 0, n:n + 1], ms[:, 0, n:n + 1], eps_rms[:, 0:1], S["rs1"])
                    elif kind == "route":
                        wait("ms2", n + 1)
                        rsqrt(rs[:, 1, n:n + 1], ms[:, 1, n:n + 1], eps_rms[:, 0:1], S["rs2"])
                    elif kind == "sum":
                        wait("u", n + 1)
                        then(pool.tensor_tensor(obuf[:, n, :], obuf[:, n, :], modB[:, 2, :], ALU.mult))
                        pool.tensor_tensor(obuf[:, n, :], obuf[:, n, :], x1[:, n, :], ALU.add).then_inc(S["o"], 1)
                assert all(chain[g] == POOL_CHAIN[g] for g in chain), chain

            part("first", 0)
            with pool.Fori(0, B - 1) as b:
                part("rows", b)
            part("last", B - 1)

        @block.tensor
        def _(pe):
            def three_pass(o, hi, lo, whi, wlo, first, last):
                pe.matmul(o, hi, whi, start=first, stop=False)
                pe.matmul(o, hi, wlo, start=False, stop=False)
                return pe.matmul(o, lo, whi, start=False, stop=last)

            def part(seg, b):
                r = 0
                def wait(name, k):
                    pe.wait_ge(S[name], (b + r) * N[name] + k + START.get(name, 0))

                def take(kind, n, **needs):
                    for signal, k, ahead in before[seg, kind, n]:
                        if signal not in needs:
                            pe.wait_ge(S[signal], (b + ahead) * N[signal] + k + START.get(signal, 0))
                        elif ahead == r:
                            needs[signal] = max(needs[signal], k)
                    for name, k in needs.items():
                        wait(name, k)
                    return of(seg, kind, n)

                if seg != "first":
                    wait("u", 0)
                for r, group, kind, n in SEG[seg]:
                    if kind == "weights":
                        pe.wait_ge(s_modA, (b + r) * 48 + 48)
                        o = take("bias", 0)
                        for k in range(KB):
                            i = pe.matmul(o[:, 0:QKV], modc[:, 0, k:k + 1].to_broadcast([P, P]), Wqkv[:, k, :],
                                          start=(k == 0), stop=(k == KB - 1))
                        i.then_inc(S["bias_pe"], 1)
                    elif kind == "mod":
                        pe.wait_ge(s_setV, V_CSL)
                        for n in range(3):
                            for k in range(KB):
                                i = pe.matmul(bank[n][0:B, :], csl[:, k, :], wm_st[:, k, n * CH:(n + 1) * CH],
                                              start=(k == 0), stop=(k == KB - 1))
                        i.then_inc(s_setP, 1)
                    elif kind == "prep" and n == 0:
                        pe.wait_ge(l_ffn, 96)
                        pe.wait_ge(s_const, 3)
                        for d in range(KB):
                            for k in range(KB):
                                i = pe.transpose(bank[3][:, (d * KB + k) * P:(d * KB + k + 1) * P],
                                                 fwv_st[:, k, d * P:(d + 1) * P], ident[:])
                        i.then_inc(s_setP, 1)
                    elif kind == "prep" and n == 1:
                        pe.wait_ge(s_setV, V_FWVT)
                        for k in range(KB):
                            for d in range(KB):
                                pe.matmul(bank[k][:, 0:C], fwvT[:, d, k * P:(k + 1) * P], fwo_st[:, d, :],
                                          start=(d == 0), stop=(d == KB - 1))
                        for d in range(KB):
                            i = pe.matmul(bank[2][:, 0:C], bvcol[:, d:d + 1].to_broadcast([P, P]), fwo_st[:, d, :],
                                          start=(d == 0), stop=(d == KB - 1))
                        i.then_inc(s_setP, 1)
                    elif kind == "xT":
                        wait("xn", n + 1)
                        o = take("xT", n)
                        for k in range(KB):
                            i = pe.transpose(o[:, k * P:(k + 1) * P], xn[:, n, k * P:(k + 1) * P], ident[:])
                        i.then_inc(S["xT"], 1)
                    elif kind == "qkv":
                        if n == 0:
                            wait("wq", 1)
                        o = take("qkv", n, xlo=n + 1)
                        for k in range(KB):
                            i = three_pass(o[:, 0:QKV], fTh[:, n % TPC, k, :], fTl[:, n % TPC, k, :], Wqhi[:, k, :], Wqlo[:, k, :],
                                           k == 0, k == KB - 1)
                        i.then_inc(S["qkv"], 1)
                    elif kind == "stackT":
                        if n % TPC == 0:
                            wait("sthi", n // TPC + 1)
                            wait("stlo", n // TPC + 1)
                        o = take("kTp", n)
                        for h in range(H):
                            at = kst_head(h)
                            i = pe.transpose(o[0:KR, h * P:(h + 1) * P], Kst[:, n % TPC, at:at + KR], ident[:])
                        i.then_inc(S["kTp"], 1)
                        o = take("qTp", n)
                        for q in range(2):
                            i = pe.transpose(o[0:QP, q * P:(q + 1) * P], Qst[:, n % TPC, 2 * q:2 * q + 2, :].rearrange(
                                "p h d -> p (h d)"), ident[:])
                        i.then_inc(S["qTp"], 1)
                    elif kind == "max":
                        qt, k0, kn, h0, hn = MAX_OF_CHUNK[n[0]][n[1]]
                        o = take("max", n, kT=qt + 1, qT=qt + 1)
                        diag = k0 + kn == (qt + 1) * P
                        for h in range(h0, h0 + hn):
                            col = (h - h0) * kn
                            i = pe.matmul(o[:, col:col + kn], QT[0:QP, h // 2, qt * P:(qt + 1) * P],
                                          KT[0:QP, h, k0:k0 + kn], start=True, stop=not diag)
                            if diag:
                                i = pe.matmul(o[:, col + kn - P:col + kn], ident_b[:], mask_qk[:],
                                              start=False, stop=True)
                        i.then_inc(S["sc"], 1)
                    elif kind == "maxrow":
                        wait("mt", n + 1)
                        o = take("mtp", n)
                        for t in range(TPC):
                            i = pe.transpose(o[0:2 * H, t * P:(t + 1) * P],
                                             mt[:, n * TPC + t, :, :].rearrange("p h e -> p (h e)"), ident[:])
                        i.then_inc(S["mtp"], 1)
                    elif kind == "prob":
                        c, j, q0 = P_UNITS[n]
                        if j == 0:
                            wait("mrow", c + 1)
                        for h in range(H):
                            o = take("st", (n, h))
                            diag = j >= c * TPC
                            i = pe.matmul(o[:, 0:CH - q0], KT[:, h, j * P:(j + 1) * P],
                                          QT[:, h // 2, c * CH + q0:(c + 1) * CH], start=True, stop=not diag)
                            if diag:
                                i = pe.matmul(o[:, 0:P], ident_b[:], mask_kq[:], start=False, stop=True)
                            i.then_inc(S["st"], 1)
                    elif kind == "pv":
                        c, j, q0 = P_UNITS[n]
                        wait("p", H * (n + 1))
                        o = take("pv", c) if j == 0 else of(seg, "pv", c)
                        for h in range(H):
                            i = pe.matmul(o[h * 2 * D:(h + 1) * 2 * D, q0:CH], V[:, j, h, :],
                                          PT[c][:, n % 2, h, 0:CH - q0], start=(j == 0), stop=(q0 == CH - P),
                                          skip_group_check=True)
                        i.then_inc(S["pv"], 1)
                    elif kind == "yT":
                        wait("yTs", n + 1)
                        o = take("yTp", n)
                        for t in range(TPC):
                            i = pe.transpose(o[:, t * P:(t + 1) * P], yT[:, t * P:(t + 1) * P], ident[:])
                        i.then_inc(S["yTp"], 1)
                    elif kind == "ynT":
                        o = take("ynTp", n, ytm=n + 1)
                        for t in range(TPC):
                            i = pe.transpose(o[0:H * D + 1, t * P:(t + 1) * P], ytm[:, t, :], ident[:])
                        i.then_inc(S["ynTp"], 1)
                    elif kind == "wo":
                        if n == 0:
                            wait("biasq", 1)
                        o = take("wo", n, yn=n // TPC + 1)
                        pe.matmul(o[:, 0:C], yT65[:, n, :], Wo_b[:], start=True, stop=True).then_inc(S["wo"], 1)
                    elif kind == "hT":
                        wait("h", n + 1)
                        o = take("hTp", n)
                        for k in range(KB):
                            i = pe.transpose(o[:, k * P:(k + 1) * P], hbuf[:, n, k * P:(k + 1) * P], ident[:])
                        i.then_inc(S["hTp"], 1)
                    elif kind == "a":
                        o = take("a", n, hlo=n + 1)
                        for k in range(KB):
                            i = three_pass(o[:, 0:W1N], fTh[:, n % TPC, k, :], fTl[:, n % TPC, k, :], W1hi[:, k, :], W1lo[:, k, :],
                                           k == 0, k == KB - 1)
                        i.then_inc(S["a"], 1)
                    elif kind == "h2T":
                        wait("h2", n + 1)
                        o = take("h2Tp", n)
                        for k in range(KB):
                            i = pe.transpose(o[:, k * P:(k + 1) * P], h2[:, n, k * P:(k + 1) * P], ident[:])
                        i.then_inc(S["h2Tp"], 1)
                    elif kind in ("gate", "up"):
                        c, f = n
                        if n == (c, 0) and kind == "gate":
                            wait("h2lo", (c + 1) * TPC)
                        cols = slice(c * CH, (c + 1) * CH)
                        blk = FB + f if kind == "up" else f if f < FB else 2 * FB
                        o = take(kind, n)
                        for k in range(KB):
                            pe.matmul(o[:], guhi[:, k, blk, :], gTh[:, k, cols], start=(k == 0), stop=False)
                            pe.matmul(o[:], guhi[:, k, blk, :], gTl[:, k, cols], start=False, stop=False)
                            i = pe.matmul(o[:], gulo[:, k, blk, :], gTh[:, k, cols], start=False,
                                          stop=(k == KB - 1))
                        i.then_inc(S[kind], 1)
                    elif kind == "down":
                        c, t = n // TPC, n % TPC
                        o = take("down", n)[:, 0:C]
                        cols = slice(t * P, (t + 1) * P)
                        if t == 0:
                            wait("fflo", c * (FB + 1) + FB - 1)
                        for f in range(FB):
                            if t == 0 and f == FB - 1:
                                wait("fflo", c * (FB + 1) + FB)
                            three_pass(o, ffhi[:, f, cols], fflo[:, f, cols], wdhi[:, f, :], wdlo[:, f, :],
                                       f == 0, False)
                        if t == 0:
                            wait("fflo", (c + 1) * (FB + 1))
                        pe.matmul(o, ffhi[:, FB, cols], wdhi[:, FB, :], start=False, stop=False)
                        pe.matmul(o, ffhi[:, FB, cols], wdlo[:, FB, :], start=False, stop=True
                                  ).then_inc(S["down"], 1)

            part("first", 0)
            with pe.Fori(0, B - 1) as b:
                part("rows", b)
            part("last", B - 1)

        @block.scalar
        def _(act):
            act.wait_ge(l_mod, 48)
            act.activation(cth, cT, ACT.Tanh, scale=0.5).then_inc(s_setA, 1)
            def part(seg, b):
                r = 0
                def wait(name, k):
                    act.wait_ge(S[name], (b + r) * N[name] + k + START.get(name, 0))

                for r, group, kind, n in SEG[seg]:
                    if kind == "prep" and 2 <= n < 2 + len(pieces):
                        if n == 2:
                            act.wait_ge(l_gu, 32)
                            act.wait_ge(l_ffn, 96)
                        w, k = staged[n - 2][:, pieces[n - 2][0][1], :], pieces[n - 2][0][1]
                        act.activation(w, w, ACT.Copy, scale=n2col[:, k:k + 1]).then_inc(s_setA, 1)
                        act.wait_ge(s_setA, 2 * n - 2)
                        for src, k, blk, cols in pieces[n - 2]:
                            hi = guhi[:, k, blk, cols]
                            i = act.activation(hi, src.rearrange("p (f n) -> p f n", n=hi.shape[2]), ACT.Copy)
                        i.then_inc(s_setA, 1)
                    elif kind == "prep" and n == 2 + len(pieces):
                        act.wait_ge(l_wd, 48)
                        act.activation(wdhi[:], wd_st, ACT.Copy).then_inc(s_setA, 1)
                    elif kind == "xT":
                        wait("xT", n + 1)
                        if n >= TPC:
                            wait("qkv", n - TPC + 1)
                        act.activation(flat(fTh[:, n % TPC, :, :]), of(seg, "xT", n)[:, 0:C], ACT.Copy).then_inc(S["xhi"], 1)
                    elif kind == "split1":
                        wait("rope", n + 1)
                        if n > 0:
                            wait("qTp", n * TPC)
                        for at in (0, D):
                            act.activation(Qst[:, :, :, at:at + D].bitcast(F32R), rot[:, :, 0:H, :], ACT.Copy)
                        for at in (0, 2 * D):
                            i = act.activation(kst[:, :, :, at:at + D].bitcast(F32R), rot[:, :, H:2 * H, :], ACT.Copy)
                        i.then_inc(S["sthi"], 1)
                    elif kind == "stackT":
                        wait("kTp", n + 1)
                        act.activation(KT[:, :, n * P:(n + 1) * P],
                                       of(seg, "kTp", n)[0:KR, :].rearrange("p (h n) -> p h n", h=H), ACT.Copy
                                       ).then_inc(S["kT"], 1)
                    elif kind == "maxrow":
                        wait("mtp", n + 1)
                        for q in range(2):
                            i = act.activation(QT[QP:KR, q, n * CH:(n + 1) * CH], of(seg, "mtp", n)[0:2 * H, :], ACT.Copy)
                        i.then_inc(S["mrow"], 1)
                    elif kind == "prob":
                        c, j, q0 = P_UNITS[n]
                        if n >= 2:
                            wait("pv", n - 1)
                        for h in range(H):
                            wait("st", n * H + h + 1)
                            act.activation(PT[c][:, n % 2, h, 0:CH - q0], of(seg, "st", (n, h))[:, 0:CH - q0], ACT.Exp,
                                           scale=float(D) ** -0.5).then_inc(S["p"], 1)
                    elif kind == "ycopy":
                        wait("pv", [m + 1 for m, u in enumerate(P_UNITS) if u[0] == n][-1])
                        if n > 0:
                            wait("yTp", n)
                        act.activation(yT[:], of(seg, "pv", n)[:], ACT.Copy).then_inc(S["yTs"], 1)
                    elif kind == "ynT":
                        wait("ynTp", n + 1)
                        act.activation(yT65[:, n * TPC:(n + 1) * TPC, :].rearrange("p t n -> p (t n)"),
                                       of(seg, "ynTp", n)[0:H * D + 1, :], ACT.Copy).then_inc(S["yn"], 1)
                    elif kind == "norm2":
                        wait("h", n + 1)
                        if n > 0:
                            wait("ms1", n)
                        act.activation(sq[:, 0, :], hbuf[:, n, :], ACT.Square, scale=float(C) ** -0.5,
                                       accum_out=ms[:, 0, n:n + 1]).then_inc(S["ms1"], 1)
                    elif kind == "hT":
                        wait("hTp", n + 1)
                        if n >= TPC:
                            wait("a", n - TPC + 1)
                        act.activation(flat(fTh[:, n % TPC, :, :]), of(seg, "hTp", n)[:, 0:C], ACT.Copy).then_inc(S["hhi"], 1)
                    elif kind == "route":
                        wait("hh", n + 1)
                        if n > 0:
                            wait("ms2", n)
                        act.activation(sq[:, 1, :], hh[:, n, :], ACT.Square, scale=float(C) ** -0.5,
                                       accum_out=ms[:, 1, n:n + 1]).then_inc(S["ms2"], 1)
                        act.activation(hbuf[:, n, :], hbuf[:, n, :], ACT.Copy, scale=r_no[:, n:n + 1]
                                       ).then_inc(S["hnr"], 1)
                    elif kind == "h2T":
                        wait("h2Tp", n + 1)
                        act.activation(gTh[:, :, n * P:(n + 1) * P], by_block(of(seg, "h2Tp", n)[:, 0:C]), ACT.Copy
                                       ).then_inc(S["h2hi"], 1)
                    elif kind == "gate":
                        c, f = n
                        m = c * (FB + 1) + f
                        wait("gate", m + 1)
                        if m >= 2:
                            wait("fft", m - 1)
                        if f < FB:
                            act.activation(sil[:, m % 2, :], of(seg, "gate", n)[:], ACT.Silu).then_inc(S["sil"], 1)
                        else:
                            act.activation(sil[FR:P, m % 2, :], of(seg, "gate", n)[0:FR, :], ACT.Silu
                                           ).then_inc(S["sil"], 1)
                    elif kind == "split":
                        c, f = n
                        m = c * (FB + 1) + f
                        wait("fft", m + 1)
                        if f == 0 and c > 0:
                            wait("down", c * TPC)
                        rows = P if f < FB else FR
                        act.activation(ffhi[0:rows, f, :], fft[0:rows, m % 2, :], ACT.Copy).then_inc(S["ffhi"], 1)

            part("first", 0)
            with act.Fori(0, B - 1) as b:
                part("rows", b)
            part("last", B - 1)

        @block.vector
        def _(dve):
            done = [0]

            def setup(i):
                i.then_inc(s_setV, 1)
                done[0] += 1
                return done[0]

            def setup_then(i):
                k = setup(i)
                dve.wait_ge(s_setV, k)

            dve.wait_ge(s_setA, 1)
            setup_then(dve.scalar_tensor_tensor(csl, cth, 1.0, cT, ALU.add, ALU.mult))
            assert setup(dve.tensor_scalar(csl, csl, 0.5, None, ALU.mult)) == V_CSL
            def part(seg, b):
                r = 0
                group = "A"
                chain = {g: 0 for g in {step[1] for step in SEG[seg]}}

                def wait(name, k):
                    dve.wait_ge(S[name], (b + r) * N[name] + k + START.get(name, 0))

                def then(i):
                    i.then_inc(S["dchain" + group], 1)
                    chain[group] += 1
                    wait("dchain" + group, chain[group])


                for r, group, kind, n in SEG[seg]:
                    if kind == "weights":
                        if seg == "first":
                            dve.wait_ge(l_small, 80)
                            dve.wait_ge(s_setV, V_SETW)
                        dve.wait_ge(s_modA, (b + r) * 48 + 48)
                        for k in range(KB):
                            i = dve.tensor_scalar(Wqhi[:, k, :], Wqkv[:, k, :], modc[:, 1, k:k + 1], None, ALU.mult)
                        then(i)
                        for k in range(KB):
                            i = dve.scalar_tensor_tensor(Wqlo[:, k, :], Wqkv[:, k, :], modc[:, 1, k:k + 1],
                                                         Wqhi[:, k, :].bitcast(F32), ALU.mult, ALU.subtract)
                        i.then_inc(S["wq"], 1)
                        dve.tensor_tensor(Wo_b[:], Wo_raw[:], modA[0:H * D + 1, :], ALU.mult)
                        wait("bias_pe", 1)
                        dve.tensor_tensor(bias_q[:], of(seg, "bias", 0)[:, 0:QKV], bqkv[:], ALU.add
                                          ).then_inc(S["biasq"], 1)
                    elif kind == "setw":
                        dve.wait_ge(l_qkv, 96)
                        groups = [(wq_st[:, k, :], wk_st[:, k, :], wv_st[:, k, :], Wqkv[:, k, :]) for k in range(KB)]
                        groups += [(bb_st[:, 0:C], bb_st[:, C:C + H * D], bb_st[:, C + H * D:C + 2 * H * D], bqkv[:])]
                        for wq, wk, wv, w in groups:
                            for e in range(2):
                                dve.tensor_reduce(w[:, 0:H * D].rearrange("p (h e i) -> p e h i", h=H, e=2)[:, e],
                                                  wq.rearrange("p (h g i e) -> p e h i g", h=H, g=G, e=2)[:, e], AX.X, ALU.add)
                                dve.tensor_copy(w[:, H * D:2 * H * D].rearrange("p (h e i) -> p e h i", h=H, e=2)[:, e],
                                                wk.rearrange("p (h i e) -> p e h i", h=H, e=2)[:, e])
                            i = dve.tensor_copy(w[:, 2 * H * D:QKV], wv)
                        setup(i)
                    elif kind == "mod":
                        dve.wait_ge(s_setP, 1)
                        for n in range(3):
                            i = dve.tensor_copy(modr[:, n * CH:(n + 1) * CH], bank[n][0:B, :])
                        setup_then(i)
                        rows = modr.rearrange("b (m v n) -> b m v n", m=2, v=3)
                        dve.tensor_scalar(rows[:, :, 1, :], rows[:, :, 1, :], 1.0, None, ALU.add)
                        setup_then(dve.tensor_scalar(gsgn, rows[:, :, 2, :], 0.0, 2.0, ALU.is_ge, ALU.mult))
                        setup_then(dve.scalar_tensor_tensor(gabs, gsgn, -1.0, rows[:, :, 2, :], ALU.add, ALU.mult))
                        setup_then(dve.tensor_scalar(gabs, gabs, 0.25, None, ALU.max))
                        assert setup(dve.scalar_tensor_tensor(rows[:, :, 2, :], gsgn, -1.0, gabs, ALU.add, ALU.mult)
                                     ) == V_MOD
                    elif kind == "prep" and n == 0:
                        dve.wait_ge(s_setP, 2)
                        assert setup(dve.tensor_copy(flat(fwvT[:]), bank[3][:])) == V_FWVT
                    elif kind == "prep" and n == 1:
                        dve.wait_ge(s_setP, 3)
                        for k in range(KB):
                            dve.tensor_scalar(w1_st[:, k, 0:C], bank[k][:, 0:C], n1col[:, k:k + 1], None, ALU.mult)
                            dve.memset(w1_st[:, k, C + 1:C + 2], 0.0)
                        setup_then(dve.tensor_copy(b1[:], bank[2][:, 0:C]))
                        setup_then(dve.tensor_copy(W1hi[:], w1_st[:]))
                        dve.tensor_tensor(W1lo[:], w1_st[:], W1hi[:].bitcast(F32), ALU.subtract)
                    elif kind == "prep" and n == 3 + len(pieces):
                        dve.wait_ge(s_setG, 1 + len(pieces))
                        dve.tensor_copy(tick[:], brout[:]).then_inc(S["u"], 1)
                    elif kind == "stats":
                        dve.wait_ge(s_x[n], (b + r) * 16 + 16)
                        ts = range(n * TPC, (n + 1) * TPC)
                        for t in ts:
                            i = dve.bn_stats(st1[:, t, :], xbuf[:, t, :])
                        then(i)
                        dve.memset(tick[:], 0.0)
                        for t in ts:
                            i = dve.bn_aggr(mv1[:, t, :], st1[:, t, :])
                        i.then_inc(S["mv1"], 1)
                    elif kind == "norm1":
                        wait("rstd1", n // TPC + 1)
                        dve.tensor_scalar(xn[:, n, :], xbuf[:, n, :], mv1[:, n, 0:1], rstd1[:, n:n + 1],
                                          ALU.subtract, ALU.mult).then_inc(S["xn"], 1)
                    elif kind == "xlo":
                        wait("xhi", n + 1)
                        dve.tensor_tensor(flat(fTl[:, n % TPC, :, :]), of(seg, "xT", n)[:, 0:C],
                                          flat(fTh[:, n % TPC, :, :]).bitcast(F32), ALU.subtract).then_inc(S["xlo"], 1)
                    elif kind == "qkvb":
                        if n == 0:
                            wait("biasq", 1)
                        wait("qkv", n + 1)
                        o = of(seg, "qkv", n)
                        dve.tensor_tensor(qk[:, n % TPC, :, :, :].rearrange("p h e i -> p (h e i)"),
                                          o[:, 0:2 * H * D], bias_q[:, 0:2 * H * D], ALU.add)
                        dve.tensor_tensor(V[:, n, :, 0:D], o[:, 2 * H * D:QKV].rearrange("p (h d) -> p h d", h=H),
                                          bias_q[:, 2 * H * D:QKV].rearrange("p (h d) -> p h d", h=H), ALU.add
                                          ).then_inc(S["qkvb"], 1)
                    elif kind == "rope":
                        if seg == "first" and n == 0:
                            dve.wait_ge(l_small, 80)
                        wait("qkvb", (n + 1) * TPC)
                        if n > 0:
                            wait("sthi", n)
                            wait("qTp", n * TPC)
                        ts = slice(n * TPC, (n + 1) * TPC)
                        cs = cos_t[:, ts, :].unsqueeze(2).to_broadcast([P, TPC, 2 * H, HALF])
                        sn = sin_t[:, ts, :].unsqueeze(2).to_broadcast([P, TPC, 2 * H, HALF])
                        ev, od = qk[:, :, :, 0, :], qk[:, :, :, 1, :]
                        for m, (u, v) in enumerate(((ev, cs), (od, sn), (ev, sn), (od, cs))):
                            i = dve.tensor_tensor(rt[:, m], u, v, ALU.mult)
                        then(i)
                        dve.tensor_tensor(rot[:, :, :, 0:HALF], rt[:, 0], rt[:, 1], ALU.subtract)
                        dve.tensor_tensor(rot[:, :, :, HALF:D], rt[:, 2], rt[:, 3], ALU.add).then_inc(S["rope"], 1)
                    elif kind == "split1":
                        wait("sthi", n + 1)
                        dve.tensor_tensor(Qst[:, :, :, 2 * D:3 * D].bitcast(F32R), rot[:, :, 0:H, :],
                                          Qst[:, :, :, 0:D], ALU.subtract)
                        dve.tensor_tensor(kst[:, :, :, D:2 * D].bitcast(F32R), rot[:, :, H:2 * H, :],
                                          kst[:, :, :, 0:D], ALU.subtract).then_inc(S["stlo"], 1)
                    elif kind == "qT":
                        wait("qTp", n + 1)
                        dve.tensor_copy(QT[0:QP, :, n * P:(n + 1) * P],
                                        by_block(of(seg, "qTp", n)[0:QP, 0:2 * P])).then_inc(S["qT"], 1)
                    elif kind == "max":
                        qt, k0, kn, h0, hn = MAX_OF_CHUNK[n[0]][n[1]]
                        wait("sc", max_index(*n) + 1)
                        dst = mx[:, qt, h0:h0 + hn] if qt < TPC else mxp[:, qt, h0:h0 + hn, k0 // CH]
                        dve.tensor_reduce(dst, of(seg, "max", n)[:, 0:hn * kn].rearrange("p (h k) -> p h k", h=hn), AX.X,
                                          ALU.max).then_inc(S["mxd"], 1)
                    elif kind == "maxrow":
                        ts = slice(n * TPC, (n + 1) * TPC)
                        wait("mxd", max_index(n, len(MAX_OF_CHUNK[n])))
                        if n > 0:
                            then(dve.tensor_reduce(mx[:, ts, :], mxp[:, ts, :, :], AX.X, ALU.max))
                        then(dve.tensor_scalar(mt[:, ts, :, 0].bitcast(F32R), mx[:, ts, :], -1.0, None, ALU.mult))
                        dve.scalar_tensor_tensor(mt[:, ts, :, 1].bitcast(F32R), mx[:, ts, :], -1.0,
                                                 mt[:, ts, :, 0], ALU.mult, ALU.subtract).then_inc(S["mt"], 1)
                    elif kind == "yT":
                        wait("yTp", n + 1)
                        if n > 0:
                            wait("ynTp", n)
                        o = of(seg, "yTp", n)[:].rearrange("p (t h d) -> p t h d", t=TPC, h=H)
                        then(dve.reciprocal(rc[:], o[:, :, :, D]))
                        dve.tensor_tensor(ytm[:, :, 0:H * D].rearrange("p t (h d) -> p t h d", h=H), o[:, :, :, 0:D],
                                          rc[:].unsqueeze(3).to_broadcast([P, TPC, H, D]), ALU.mult
                                          ).then_inc(S["ytm"], 1)
                    elif kind == "x1":
                        if n == 0:
                            wait("o", 0)
                        wait("wo", n + 1)
                        dve.tensor_tensor(x1[:, n, :], of(seg, "wo", n)[:, 0:C], xbuf[:, n, :], ALU.add
                                          ).then_inc(S["x1"], 1)
                        wait("x1", n + 1)
                        then(dve.bn_stats(st[:, n, :], x1[:, n, :]))
                        dve.memset(tick[:], 0.0)
                        dve.bn_aggr(mv2[:, n, :], st[:, n, :]).then_inc(S["mv2"], 1)
                    elif kind == "norm2":
                        wait("rstd2", n + 1)
                        dve.tensor_scalar(hbuf[:, n, :], x1[:, n, :], mv2[:, n, 0:1], rstd2[:, n:n + 1],
                                          ALU.subtract, ALU.mult).then_inc(S["xh"], 1)
                    elif kind == "hlo":
                        wait("hhi", n + 1)
                        dve.tensor_tensor(flat(fTl[:, n % TPC, :, :]), of(seg, "hTp", n)[:, 0:C],
                                          flat(fTh[:, n % TPC, :, :]).bitcast(F32), ALU.subtract).then_inc(S["hlo"], 1)
                    elif kind == "route":
                        wait("a", n + 1)
                        wait("rs1", n + 1)
                        wait("hb", n + 1)
                        o = of(seg, "a", n)
                        dve.tensor_scalar(r_no[:, n:n + 1], o[:, C:C + 1], brout[:], 0.0, ALU.add, ALU.is_le)
                        dve.tensor_scalar(r_yes[:, n:n + 1], o[:, C:C + 1], brout[:], 0.0, ALU.add, ALU.is_gt)
                        dve.scalar_tensor_tensor(hh[:, n, :], o[:, 0:C], rs[:, 0, n:n + 1], hh[:, n, :],
                                                 ALU.mult, ALU.add).then_inc(S["hh"], 1)
                    elif kind == "h2":
                        wait("rs2", n + 1)
                        dve.tensor_scalar(h2[:, n, :], hh[:, n, :], rs[:, 1, n:n + 1], None, ALU.mult
                                          ).then_inc(S["h2"], 1)
                        wait("hnr", n + 1)
                        dve.scalar_tensor_tensor(hbuf[:, n, :], hh[:, n, :], r_yes[:, n:n + 1], hbuf[:, n, :],
                                                 ALU.mult, ALU.add).then_inc(S["hsel"], 1)
                    elif kind == "h2lo":
                        wait("h2hi", n + 1)
                        cols = slice(n * P, (n + 1) * P)
                        dve.tensor_tensor(gTl[:, :, cols], by_block(of(seg, "h2Tp", n)[:, 0:C]),
                                          gTh[:, :, cols].bitcast(F32), ALU.subtract).then_inc(S["h2lo"], 1)
                    elif kind == "fft":
                        c, f = n
                        m = c * (FB + 1) + f
                        wait("sil", m + 1)
                        if m >= 2:
                            wait("fflo", m - 1)
                        if f < FB:
                            wait("up", c * FB + f + 1)
                            i = dve.tensor_tensor(fft[:, m % 2, :], sil[:, m % 2, :], of(seg, "up", n)[:], ALU.mult)
                        else:
                            i = dve.tensor_tensor(fft[0:FR, m % 2, :], sil[FR:P, m % 2, :], of(seg, "gate", n)[FR:P, :],
                                                  ALU.mult)
                        i.then_inc(S["fft"], 1)
                    elif kind == "split":
                        c, f = n
                        m = c * (FB + 1) + f
                        wait("ffhi", m + 1)
                        if f < FB:
                            i = dve.tensor_tensor(fflo[:, f, :], fft[:, m % 2, :], ffhi[:, f, :].bitcast(F32),
                                                  ALU.subtract)
                        else:
                            i = dve.tensor_tensor(ffhi[FR:P, FB, :], fft[0:FR, m % 2, :],
                                                  ffhi[0:FR, FB, :].bitcast(F32), ALU.subtract)
                        i.then_inc(S["fflo"], 1)
                    elif kind == "sum":
                        wait("down", n + 1)
                        if n == 0:
                            dve.wait_ge(s_out, 16 * NC * b + 1)
                        dve.scalar_tensor_tensor(obuf[:, n, :], of(seg, "down", n)[:, 0:C], r_yes[:, n:n + 1],
                                                 hbuf[:, n, :], ALU.mult, ALU.add).then_inc(S["u"], 1)
                assert all(chain[g] == DVE_CHAIN[g] for g in chain), chain

            part("first", 0)
            with dve.Fori(0, B - 1) as b:
                part("rows", b)
            part("last", B - 1)



_INS = ["L0_attn_x", "L0_attn_Wq", "L0_attn_bq", "L0_attn_Wk", "L0_attn_bk", "L0_attn_Wv", "L0_attn_bv", "L0_attn_Wo",
        "L0_attn_bo", "L0_ffn_w_router", "L0_ffn_b_router", "L0_ffn_norm1_w", "L0_ffn_wv", "L0_ffn_bv", "L0_ffn_wo",
        "L0_ffn_norm2_w", "L0_ffn_w_gate", "L0_ffn_w_up", "L0_ffn_w_down", "L0_c", "L0_wmod"]


def rope_tables():
    inv = (1.0 / 10000.0 ** (np.arange(HALF, dtype=np.float32) * 2.0 / D)).astype(np.float32)
    angle = np.arange(T, dtype=np.float32)[:, None] * inv[None, :]

    def lay(a):
        return np.ascontiguousarray(a.astype(np.float32).reshape(NT, P, HALF).transpose(1, 0, 2))

    return lay(np.cos(angle)), lay(np.sin(angle))


def kernel(**inputs):
    import concourse.bacc as bacc
    from concourse.bass_utils import run_bass_kernel_spmd

    nc = bacc.Bacc("TRN2", target_bir_lowering=False, num_devices=1)
    arrays = {name: np.ascontiguousarray(inputs[name]) for name in _INS}
    arrays["L0_ffn_b_router"] = arrays["L0_ffn_b_router"].reshape(1)
    arrays["rope_cos"], arrays["rope_sin"] = rope_tables()
    args = [nc.dram_tensor(f"in_{n}", a.shape, mybir.dt.from_np(a.dtype), kind="ExternalInput").ap()
            for n, a in arrays.items()]
    out = nc.dram_tensor("out_x", (B, T, C), F32, kind="ExternalOutput").ap()
    adaln_layer(nc, *args, out)
    r = run_bass_kernel_spmd(nc, [{f"in_{n}": a for n, a in arrays.items()}], core_ids=[0])
    return r.results[0]["out_x"]
```
